# Optimizing a Trainium2 kernel written in Bass

```python
import numpy as np
import jax
import jax.numpy as jnp

def _softmax(x, axis=-1):
    return jax.nn.softmax(x, axis=axis)

def _gelu(x):
    return jax.nn.gelu(x, approximate=True)

def _silu(x):
    return jax.nn.silu(x)

def _sigmoid(x):
    return jax.nn.sigmoid(x)

def _layernorm(x, axis=-1, eps=1e-05):
    m = jnp.mean(x, axis=axis, keepdims=True)
    v = jnp.var(x, axis=axis, keepdims=True)
    return (x - m) / jnp.sqrt(v + eps)

def _scatter_add(tgt, idx, src, axis=0):
    return tgt.at[idx].add(src)

def _segment_sum(src, seg, n):
    return jax.ops.segment_sum(src, seg, n)
kernel_name = 'mk_early_fusion_d1_tok_img768_r4_4c59ec'

def setup_inputs(seed: int=0):
    np.random.seed(seed)
    _w = jnp.asarray

    def _rec_inputs():
        import jax
        import jax.numpy as jnp
        _rk = jax.random.key(seed)
        x = 7.57192e-06 + 1.00007 * jax.random.normal(jax.random.fold_in(_rk, 1), (2, 3, 128, 128), jnp.float32)
        txt = 0.000103109 + 0.277508 * jax.random.normal(jax.random.fold_in(_rk, 2), (2, 32, 192), jnp.float32)
        return (x, txt)
    x, txt = _rec_inputs()

    def _L0_tok_setup():
        import jax, jax.numpy as jnp
        import numpy as np
        QMAX = 127.0

        def fake_quant(v):
            s = jnp.maximum(jnp.max(jnp.abs(v)), 1e-08) / QMAX
            return jnp.round(jnp.clip(v / s, -QMAX, QMAX)) * s
        key = jax.random.key(seed)
        k1, k2, k3 = jax.random.split(key, 3)
        B, C, H, W = (64, 3, 224, 224)
        D, P = (192, 8)
        x = jax.random.normal(k1, (B, C, H, W), dtype=jnp.float32)
        w = jax.random.normal(k2, (D, C, P, P), dtype=jnp.float32) * 0.02
        b = jax.random.normal(k3, (D,), dtype=jnp.float32) * 0.02
        return {'x': x, 'w': w, 'b': b}
    _L0_tok_all = _L0_tok_setup()
    _L0_tok_in = {k: v for k, v in _L0_tok_all.items() if k in ('w', 'b')}
    del _L0_tok_all

    def _L0_attn_setup():
        import jax, jax.numpy as jnp
        import numpy as np
        B, L, C = (1, 384, 192)
        H, DK, DV, F = (8, 64, 96, 96)

        def central_mask_embed(n, features):
            positions = jnp.arange(-(n - 1), n)
            widths = jnp.float32(2.0) ** jnp.arange(1, features + 1, dtype=jnp.float32) - 1.0
            return (widths[None, :] > jnp.abs(positions).astype(jnp.float32)[:, None]).astype(jnp.float32)

        def relative_shift(t):
            b, h, t1, t2 = t.shape
            t = jnp.pad(t, ((0, 0), (0, 0), (0, 0), (1, 0)))
            t = t.reshape(b, h, t2 + 1, t1)[:, :, 1:, :]
            t = t.reshape(b, h, t1, t2)
            return t[..., :(t2 + 2) // 2]
        key = jax.random.key(seed)
        ks = jax.random.split(key, 9)
        s = 0.02
        return {'x': jax.random.normal(ks[0], (B, L, C), jnp.float32), 'Wq': jax.random.normal(ks[1], (C, H * DK), jnp.float32) * s, 'Wk': jax.random.normal(ks[2], (C, H * DK), jnp.float32) * s, 'Wv': jax.random.normal(ks[3], (C, H * DV), jnp.float32) * s, 'Wout': jax.random.normal(ks[4], (H * DV, C), jnp.float32) * s, 'bout': jnp.zeros((C,), jnp.float32), 'Wpos': jax.random.normal(ks[5], (F, H * DK), jnp.float32) * s, 'rel_content_bias': jax.random.normal(ks[6], (1, H, 1, DK), jnp.float32), 'rel_pos_bias': jax.random.normal(ks[7], (1, H, 1, DK), jnp.float32)}
    _L0_attn_all = _L0_attn_setup()
    _L0_attn_in = {k: v for k, v in _L0_attn_all.items() if k in ('Wq', 'Wk', 'Wv', 'Wout', 'bout', 'Wpos', 'rel_content_bias', 'rel_pos_bias')}
    del _L0_attn_all

    def _L0_ffn_setup():
        import jax, jax.numpy as jnp
        import numpy as np
        B, S, D_IN, D_HID, D_OUT = (32, 128, 192, 768, 192)
        key = jax.random.key(seed)
        k1, k2, k3, k4 = jax.random.split(key, 4)
        init_k = float(np.sqrt(1.0 / D_IN))
        init_k2 = float(np.sqrt(1.0 / D_HID))
        x = jax.random.normal(k1, (B, S, D_IN), dtype=jnp.float32)
        in_weight = jax.random.uniform(k2, (D_HID, D_IN), dtype=jnp.float32, minval=-init_k, maxval=init_k)
        in_bias = jax.random.uniform(k3, (D_HID,), dtype=jnp.float32, minval=-init_k, maxval=init_k)
        out_weight = jax.random.uniform(k4, (D_HID, D_OUT), dtype=jnp.float32, minval=-init_k2, maxval=init_k2)
        return {'x': x, 'in_weight': in_weight, 'in_bias': in_bias, 'out_weight': out_weight}
    _L0_ffn_all = _L0_ffn_setup()
    _L0_ffn_in = {k: v for k, v in _L0_ffn_all.items() if k in ('in_weight', 'in_bias', 'out_weight')}
    del _L0_ffn_all
    return {'x': x, 'txt': txt, 'L0_tok_w': _L0_tok_in['w'], 'L0_tok_b': _L0_tok_in['b'], 'L0_attn_Wq': _L0_attn_in['Wq'], 'L0_attn_Wk': _L0_attn_in['Wk'], 'L0_attn_Wv': _L0_attn_in['Wv'], 'L0_attn_Wout': _L0_attn_in['Wout'], 'L0_attn_bout': _L0_attn_in['bout'], 'L0_attn_Wpos': _L0_attn_in['Wpos'], 'L0_attn_rel_content_bias': _L0_attn_in['rel_content_bias'], 'L0_attn_rel_pos_bias': _L0_attn_in['rel_pos_bias'], 'L0_ffn_in_weight': _L0_ffn_in['in_weight'], 'L0_ffn_in_bias': _L0_ffn_in['in_bias'], 'L0_ffn_out_weight': _L0_ffn_in['out_weight']}

def reference(x, txt, L0_tok_w, L0_tok_b, L0_attn_Wq, L0_attn_Wk, L0_attn_Wv, L0_attn_Wout, L0_attn_bout, L0_attn_Wpos, L0_attn_rel_content_bias, L0_attn_rel_pos_bias, L0_ffn_in_weight, L0_ffn_in_bias, L0_ffn_out_weight):
    import jax
    import jax.numpy as jnp

    def _L0_tok_ref(x, w, b):
        import jax, jax.numpy as jnp
        import numpy as np
        QMAX = 127.0

        def fake_quant(v):
            s = jnp.maximum(jnp.max(jnp.abs(v)), 1e-08) / QMAX
            return jnp.round(jnp.clip(v / s, -QMAX, QMAX)) * s
        B, C, H, W = x.shape
        D, _, P, _ = w.shape
        gh, gw = (H // P, W // P)
        xq = fake_quant(x)
        wq = fake_quant(w)
        xp = xq.reshape(B, C, gh, P, gw, P)
        out = jnp.einsum('bchpwq,dchq->bhwd', xp.transpose(0, 1, 2, 3, 4, 5), wq, optimize=True) if False else jnp.einsum('bcxpyq,dcpq->bxyd', xp, wq)
        out = out + b
        out = out.reshape(B, gh * gw, D)
        return out

    def _L0_attn_ref(x, Wq, Wk, Wv, Wout, bout, Wpos, rel_content_bias, rel_pos_bias):
        import jax, jax.numpy as jnp
        import numpy as np
        B, L, C = (1, 384, 192)
        H, DK, DV, F = (8, 64, 96, 96)

        def central_mask_embed(n, features):
            positions = jnp.arange(-(n - 1), n)
            widths = jnp.float32(2.0) ** jnp.arange(1, features + 1, dtype=jnp.float32) - 1.0
            return (widths[None, :] > jnp.abs(positions).astype(jnp.float32)[:, None]).astype(jnp.float32)

        def relative_shift(t):
            b, h, t1, t2 = t.shape
            t = jnp.pad(t, ((0, 0), (0, 0), (0, 0), (1, 0)))
            t = t.reshape(b, h, t2 + 1, t1)[:, :, 1:, :]
            t = t.reshape(b, h, t1, t2)
            return t[..., :(t2 + 2) // 2]
        b, n, _ = x.shape
        q = (x @ Wq).reshape(b, n, H, DK).transpose(0, 2, 1, 3)
        k = (x @ Wk).reshape(b, n, H, DK).transpose(0, 2, 1, 3)
        v = (x @ Wv).reshape(b, n, H, DV).transpose(0, 2, 1, 3)
        q = q / jnp.float32(DK) ** 0.5
        content_logits = jnp.einsum('bhid,bhjd->bhij', q + rel_content_bias, k)
        pos = central_mask_embed(n, F)
        pos_k = (pos @ Wpos).reshape(2 * n - 1, H, DK).transpose(1, 0, 2)
        pos_logits = jnp.einsum('bhid,hjd->bhij', q + rel_pos_bias, pos_k)
        pos_logits = relative_shift(pos_logits)
        attn = jax.nn.softmax(content_logits + pos_logits, axis=-1)
        out = jnp.einsum('bhij,bhjd->bhid', attn, v)
        out = out.transpose(0, 2, 1, 3).reshape(b, n, H * DV)
        return out @ Wout + bout

    def _L0_ffn_ref(x, in_weight, in_bias, out_weight):
        import jax, jax.numpy as jnp
        import numpy as np
        B, S, D_IN, D_HID, D_OUT = (32, 128, 192, 768, 192)
        lead = x.shape[:-1]
        xt = x.reshape(-1, in_weight.shape[1])
        h = jax.nn.gelu(jnp.einsum('td,hd->th', xt, in_weight) + in_bias, approximate=False)
        out = jnp.einsum('th,ho->to', h, out_weight)
        return out.reshape(*lead, out_weight.shape[1])
    h = _L0_tok_ref(x, L0_tok_w, L0_tok_b)
    h = jnp.concatenate([h, txt], axis=1)
    h = h + _L0_attn_ref(_layernorm(h, axis=-1), L0_attn_Wq, L0_attn_Wk, L0_attn_Wv, L0_attn_Wout, L0_attn_bout, L0_attn_Wpos, L0_attn_rel_content_bias, L0_attn_rel_pos_bias)
    h = h + _L0_ffn_ref(_layernorm(h, axis=-1), L0_ffn_in_weight, L0_ffn_in_bias, L0_ffn_out_weight)
    return h

_drawn_inputs = setup_inputs


def setup_inputs(seed=0):
    import zlib

    import numpy as np

    out = dict(_drawn_inputs(seed))
    spreads = {'L0_attn_bout': (0.0, 0.1)}
    factors = {'L0_attn_Wq': 5.974, 'L0_attn_Wpos': 3.306, 'L0_attn_rel_pos_bias': 3.265}
    for name, (base, spread) in spreads.items():
        noise = np.random.default_rng([zlib.crc32(name.encode()), seed]).standard_normal(out[name].shape)
        drawn = base * np.exp(spread * noise) if base else spread * noise
        out[name] = jnp.asarray(drawn.astype(out[name].dtype))
    for name, factor in factors.items():
        out[name] = (out[name] * factor).astype(out[name].dtype)
    return out
```

```python
from contextlib import ExitStack

import concourse.bass as bass
from concourse import mybir

F32 = mybir.dt.float32
BF16 = mybir.dt.bfloat16
ALU = mybir.AluOpType
ACT = mybir.ActivationFunctionType
AX_X = mybir.AxisListType.X

QMAX = 127.0
ROUND = 1.5 * 2.0 ** 23
BIG = 3.0e38
EPS = 1e-5


def plan_items(B, H, PAIRS, TILES, CHUNKS, HID, VH, LAG):
    items = []
    turn = [0]

    def add(kind, *key, eng=None):
        if eng is None:
            eng = "AV"[turn[0] % 2]
            turn[0] += 1
        items.append((kind, key, eng))

    add("posg", eng="V")
    add("peak", eng="V")
    add("scale", eng="V")
    for b in range(B):
        for t in range(TILES):
            add("tok", b, t, eng="V")
    for t in range(TILES):
        add("xnT", 0, t, eng="A")
    for p in range(PAIRS):
        add("q", 0, p)
    for b in range(1, B):
        for t in range(TILES):
            add("xnT", b, t, eng="A")
    for p in range(PAIRS):
        add("k", 0, p)
    add("a", 0, eng="V")
    big = [("q", 1, p) for p in range(PAIRS)] + [("k", 1, p) for p in range(PAIRS)]
    big += [("v", 0, t, n) for t in range(TILES) for n in range(VH)]
    for it in big[:3]:
        add(*it)
    big = big[3:]
    for t in range(TILES):
        add("aT", 0, t)
    for c in range(CHUNKS):
        add("T", 0, c)
        if c % 3 != 2 and big:
            add(*big.pop(0))
    for it in big:
        add(*it)
    add("a", 1, eng="V")
    for t in range(TILES):
        for n in range(VH):
            add("v", 1, t, n)
    for t in range(TILES):
        add("aT", 1, t)

    G = B * H * TILES
    half = H * TILES
    tail = [("y", t) for t in range(TILES)] + [None] * 3 + [("x2T", t) for t in range(TILES)]
    tail += [("f1", m) for m in range(HID)] + [None] + [("f2", t) for t in range(TILES)]
    after = {}
    for i, it in enumerate(tail):
        if it is not None:
            after[half + LAG + 3 + i] = it

    def add_tail(it, b):
        kind = it[0]
        add(kind, b, it[1], eng={"y": "V", "x2T": "A", "f1": "A", "f2": "V"}[kind])

    late = []
    for g in range(G + LAG + 1):
        if g < G:
            add("s", g, eng="V")
        if g < CHUNKS:
            add("T", 1, g)
        x = g - LAG
        if 0 <= x < G:
            add("x", x)
        if x >= TILES and x % TILES == 0:
            add("o", x // TILES - 1)
        if g in after:
            add_tail(after[g], 0)
            after.pop(g)
    for g in sorted(after):
        add_tail(after[g], 0)
    for it in tail:
        if it is not None:
            add_tail(it, 1)
    return items


def early_fusion_kernel(nc, xpat, txt, wpat, tok_b, wq, wk, wv, wout, bout, wpos, cols, w1, w2,
                        ident, bucket_sum, bucket_mask, out):
    KP, KT, BP = xpat.shape
    B, NT, D = txt.shape
    NP = BP // B
    N = NP + NT
    TP = 96
    TILES = N // TP
    LASTP = NP - (TILES - 1) * TP
    HDK = wq.shape[2]
    PAIRS = HDK // 128
    DK = 64
    H = HDK // DK
    HDV = wv.shape[2]
    DV = HDV // H
    HID = w1.shape[2] // 128
    F = wpos.shape[0]
    NB = bucket_sum.shape[1]
    REL = 2 * N - 1
    SPLIT = 3
    KA = 96
    U = 16
    CHUNKS = N // U
    TW = N + U - 1
    PITCH = 2 * N
    GRP = 3
    NGRP = CHUNKS // GRP
    SLOTS = 2
    VH = 2
    VW = HDV // VH
    LAG = 4
    G = B * H * TILES
    assert TILES * TP == N and U * H == 128 and SPLIT * NB <= KA and DK == 64 and NGRP % TILES == 0

    items = plan_items(B, H, PAIRS, TILES, CHUNKS, HID, VH, LAG)
    index = {(kind, *key): i for i, (kind, key, _) in enumerate(items)}

    with ExitStack() as ctx:
        def sb(name, shape, dt=F32):
            return ctx.enter_context(nc.sbuf_tensor(name, shape, dt))

        def sem(name):
            return ctx.enter_context(nc.semaphore(name))

        psum = ctx.enter_context(nc.psum_tensor("psum", [128, 8, 512], F32))
        skew = [nc.dram_tensor(f"skew{b}", [H, N, PITCH], F32, kind="Internal") for b in range(B)]

        early = sb("early", [128, max(KT * BP + KT * D, HID * N)])
        xf = early[0:KP, 0:KT * BP].rearrange("p (k n) -> p k n", k=KT)
        wf = early[0:KP, KT * BP:KT * BP + KT * D].rearrange("p (k n) -> p k n", k=KT)
        hidden = early[:, 0:HID * N].rearrange("p (m n) -> p m n", m=HID)
        x8 = sb("x8", [KP, KT, BP], BF16)
        w8 = sb("w8", [KP, KT, D], BF16)
        idf = sb("idf", [128, 128])
        idb = sb("idb", [TP, TP], BF16)
        ones = sb("ones", [1, TP])
        peaks = sb("peaks", [KP, 2])
        srow = sb("srow", [1, 8])
        scales = sb("scales", [TP, 3])
        tokb = sb("tokb", [TP, D])
        boutb = sb("boutb", [TP, D])
        colv = sb("colv", [128, cols.shape[1]])
        wq_s = sb("wq_s", [KP, KT, HDK])
        wk_s = sb("wk_s", [KP, KT, HDK])
        wv_s = sb("wv_s", [KP, KT, HDV])
        wo_s = sb("wo_s", [DV, H, D])
        w1_s = sb("w1_s", [KP, KT, HID * 128])
        w2_s = sb("w2_s", [128, HID, D])
        wpos_s = sb("wpos_s", [F, HDK])
        bsum = sb("bsum", [F, NB])
        maskf = sb("maskf", [SPLIT * NB, REL])
        mask = sb("mask", [KA, REL + 1], BF16)
        gpos = sb("gpos", [128, PAIRS, 2 * NB])
        h = sb("h", [TP, B * TILES, D])
        xn = sb("xn", [TP, B * TILES, D])
        stats = sb("stats", [TP, B * TILES, 6])
        meanvar = sb("meanvar", [TP, B * TILES, 2])
        vareps = sb("vareps", [TP, B * TILES])
        neghalf = sb("neghalf", [TP, TILES])
        rstd = sb("rstd", [TP, B * TILES])
        xnT = sb("xnT", [KP, KT, B * N])
        qc = sb("qc", [128, PAIRS, B * N])
        qp = sb("qp", [128, PAIRS, B * N])
        kz = sb("kz", [128, H, B * N])
        v = sb("v", [TP, B * TILES, HDV])
        arow = sb("arow", [TP, TILES * H, NB])
        a3 = sb("a3", [TP, TILES * H, KA], BF16)
        aT = sb("aT", [KA, CHUNKS, 128], BF16)
        tpos = sb("tpos", [128, SLOTS * GRP, TW])
        att = sb("att", [TP, B, TILES, H, N])
        nmax = sb("nmax", [TP, G])
        esum = sb("esum", [TP, G])
        rsum = sb("rsum", [TP, G])
        attT = sb("attT", [TP, 2, TILES, N])
        oT1 = sb("oT1", [DV, H, N])
        oT = [qp[0:DV, :, :].rearrange("p a n -> p (a n)")[:, 0:H * N].rearrange("p (h n) -> p h n", h=H), oT1]

        filled = sem("filled")
        emptied = {"A": sem("emptied_by_act"), "V": sem("emptied_by_dve")}
        ld = {n: sem("ld_" + n) for n in ("x0", "x1", "w", "id", "rows", "txt", "cols", "pos", "mask", "wq", "wk",
                                          "wv", "wo", "w1", "w2")}
        peak_found = sem("peak_found")
        scale_found = sem("scale_found")
        x_scaled = sem("x_scaled")
        x_shifted = sem("x_shifted")
        x_rounded = sem("x_rounded")
        zeroed = sem("zeroed")
        id_cast = sem("id_cast")
        mask_cast = sem("mask_cast")
        ones_set = sem("ones_set")
        ln_step = sem("ln_step")
        var_ready = sem("var_ready")
        rstd_ready = sem("rstd_ready")
        xn_ready = sem("xn_ready")
        bout_added = sem("bout_added")
        a_step = sem("a_step")
        a_split = sem("a_split")
        tpos_out = [sem(f"tpos_out{i}") for i in range(B * NGRP)]
        pos_in = [sem(f"pos_in{i}") for i in range(B * TILES)]
        exp_done = sem("exp_done")
        recip_done = sem("recip_done")
        weights_done = sem("weights_done")
        out_done = sem("out_done")

        emptied_upto = []
        count = {"A": 0, "V": 0}
        for _, _, e in items:
            count[e] += 1
            emptied_upto.append(count[e])

        def wait_filled(eng, *key):
            eng.wait_ge(filled, index[key] + 1)

        def wait_emptied(eng, *key):
            i = index[key]
            eng.wait_ge(emptied[items[i][2]], emptied_upto[i])

        def patches_of(t):
            return TP if t < TILES - 1 else LASTP

        def att_tile(g):
            bh, t = divmod(g, TILES)
            b, hh = divmod(bh, H)
            return att[:, b, t, hh, :]

        ctx.enter_context(nc.allow_non_contiguous_dma(reason="rows of a few hundred bytes"))
        late_root = sum(kind == "s" for kind, _, _ in items[:index["y", 0, TILES - 1]]) - 1
        block = ctx.enter_context(nc.Block())

        @block.sync
        def _(sp):
            for k in range(KT):
                sp.dma_start(xf[:, k, :], xpat[:, k, :]).then_inc(ld[f"x{k}"], 16)
            sp.dma_start(wf, wpat).then_inc(ld["w"], 16)
            sp.dma_start(wq_s[:], wq).then_inc(ld["wq"], 16)
            sp.dma_start(wk_s[:], wk).then_inc(ld["wk"], 16)
            sp.dma_start(wv_s[:], wv).then_inc(ld["wv"], 16)
            sp.dma_start(wo_s[:], wout).then_inc(ld["wo"], 16)
            sp.dma_start(w1_s[:], w1).then_inc(ld["w1"], 16)
            sp.dma_start(w2_s[:], w2).then_inc(ld["w2"], 16)

            def send(b, grp):
                for c in range(GRP * grp, GRP * grp + GRP):
                    wait_emptied(sp, "T", b, c)
                slot = (b * NGRP + grp) % SLOTS
                for c in range(GRP * grp, GRP * grp + GRP):
                    first = N - 1 - (U * c + U - 1)
                    dst = bass.AP(skew[b], U * c * PITCH + first, [[PITCH, U], [N * PITCH, H], [1, TW]])
                    sp.dma_start(dst, tpos[:, slot * GRP + c % GRP, :]).then_inc(tpos_out[b * NGRP + grp], 16)

            def fetch(b, t):
                per = NGRP // TILES
                for grp in range(per * t, per * t + per):
                    sp.wait_ge(tpos_out[b * NGRP + grp], 16 * GRP)
                src = bass.AP(skew[b], t * TP * PITCH + N - 1 - t * TP,
                              [[PITCH - 1, TP], [N * PITCH, H], [1, N]])
                sp.dma_start(att[:, b, t, :, :], src).then_inc(pos_in[b * TILES + t], 16)

            for b in range(B):
                per = NGRP // TILES
                for grp in range(NGRP):
                    send(b, grp)
                    if grp >= per and grp % per == 0:
                        fetch(b, grp // per - 1)
                fetch(b, TILES - 1)
            for b in range(B):
                for t in range(TILES):
                    wait_emptied(sp, "f2", b, t)
                    sp.dma_start(out[b, t * TP:(t + 1) * TP, :], xn[:, b * TILES + t, :]).then_inc(out_done, 16)
            sp.wait_ge(out_done, 16 * B * TILES)

        @block.gpsimd
        def _(pool):
            nc.gpsimd.memset(ones[:], 1.0).then_inc(ones_set, 1)
            nc.gpsimd.memset(gpos[:], 0.0).then_inc(zeroed, 1)
            nc.gpsimd.memset(a3[:], 0.0).then_inc(zeroed, 1)
            nc.gpsimd.memset(mask[:], 0.0).then_inc(zeroed, 1)
            nc.gpsimd.memset(neghalf[:], -0.5).then_inc(zeroed, 1)
            pool.wait_ge(ld["id"], 16)
            nc.gpsimd.tensor_copy(idb[:], idf[0:TP, 0:TP]).then_inc(id_cast, 1)
            pool.wait_ge(id_cast, 1)
            kz2 = kz[:].rearrange("p (a two) n -> p a two n", two=2)
            nc.gpsimd.memset(kz2[0:64, :, 1, :], 0.0).then_inc(zeroed, 1)
            pool.wait_ge(zeroed, 5)
            nc.gpsimd.memset(kz2[64:128, :, 0, :], 0.0).then_inc(zeroed, 1)
            pool.wait_ge(ld["mask"], 16)
            pool.wait_ge(zeroed, 6)
            nc.gpsimd.tensor_copy(mask[0:SPLIT * NB, 0:REL], maskf[:]).then_inc(mask_cast, 1)

            def root(b, nth):
                pool.wait_ge(var_ready, nth + 1)
                a, z = b * TILES, (b + 1) * TILES
                nc.gpsimd.tensor_tensor(rstd[:, a:z], vareps[:, a:z], neghalf[:], ALU.pow).then_inc(rstd_ready, 1)

            for b in range(B):
                root(b, b)
            for n in range(B * TILES):
                pool.wait_ge(xn_ready, n + 1)
                nc.gpsimd.tensor_tensor(h[:, n, :], h[:, n, :], boutb[:], ALU.add).then_inc(bout_added, 1)
            for g in range(G):
                if g == late_root:
                    root(0, B)
                pool.wait_ge(recip_done, g + 1)
                e = att_tile(g)
                nc.gpsimd.tensor_scalar(e, e, rsum[:, g:g + 1], 1.0, ALU.mult, ALU.mult).then_inc(weights_done, 1)
            for b in range(1, B):
                root(b, B + b)

        @block.scalar
        def _(act):
            act.dma_start(idf[:], ident).then_inc(ld["id"], 16)
            act.dma_start(tokb[:], tok_b.partition_broadcast(TP)).then_inc(ld["rows"], 16)
            act.dma_start(boutb[:], bout.partition_broadcast(TP)).then_inc(ld["rows"], 16)
            for b in range(B):
                act.dma_start(h[LASTP:TP, b * TILES + TILES - 1, :], txt[b]).then_inc(ld["txt"], 16)
            act.dma_start(wpos_s[:], wpos).then_inc(ld["pos"], 16)
            act.dma_start(bsum[:], bucket_sum).then_inc(ld["pos"], 16)
            act.dma_start(colv[:], cols).then_inc(ld["cols"], 16)
            act.dma_start(maskf[:], bucket_mask).then_inc(ld["mask"], 16)

            act.wait_ge(x_shifted, 1)
            nc.scalar.activation(w8[:], wf, ACT.Copy, bias=-ROUND).then_inc(x_rounded, 1)
            for b in range(B):
                act.wait_ge(x_shifted, 2 + b)
                nc.scalar.activation(x8[:, :, b * NP:(b + 1) * NP], xf[:, :, b * NP:(b + 1) * NP], ACT.Copy,
                                     bias=-ROUND).then_inc(x_rounded, 1)
            act.wait_ge(ld["cols"], 16)

            for i, (kind, key, eng) in enumerate(items):
                bank = psum[:, i % 8, :]
                if kind == "s":
                    g = key[0]
                    wait_emptied(act, "s", g)
                    nc.scalar.activation(att_tile(g), att_tile(g), ACT.Exp, bias=nmax[:, g:g + 1], scale=-1.0,
                                         accum_out=esum[:, g:g + 1]).then_inc(exp_done, 1)
                if eng != "A":
                    continue
                act.wait_ge(filled, i + 1)
                if kind in ("xnT", "x2T"):
                    b, t = key
                    c0 = b * N + t * TP
                    last = nc.scalar.copy(xnT[:, :, c0:c0 + TP],
                                          bank[0:KP, 0:KT * TP].rearrange("p (k n) -> p k n", k=KT))
                elif kind == "q":
                    b, p = key
                    cs = slice(b * N, b * N + N)
                    nc.scalar.activation(qc[:, p, cs], bank[:, 0:N], ACT.Identity, bias=colv[:, p:p + 1],
                                         scale=DK ** -0.5)
                    last = nc.scalar.activation(qp[:, p, cs], bank[:, 0:N], ACT.Identity,
                                                bias=colv[:, PAIRS + p:PAIRS + p + 1], scale=DK ** -0.5)
                elif kind == "k":
                    b, p = key
                    cs = slice(b * N, b * N + N)
                    nc.scalar.copy(kz[0:64, 2 * p, cs], bank[0:64, 0:N])
                    last = nc.scalar.copy(kz[64:128, 2 * p + 1, cs], bank[64:128, 0:N])
                elif kind == "v":
                    b, t, n = key
                    last = nc.scalar.copy(v[:, b * TILES + t, n * VW:(n + 1) * VW], bank[0:TP, 0:VW])
                elif kind == "aT":
                    b, t = key
                    if b:
                        wait_filled(act, "T", b - 1, CHUNKS - 1)
                    per = TP // U
                    last = nc.scalar.copy(
                        aT[:, per * t:per * t + per, :].rearrange("p c (u h) -> p h c u", h=H),
                        bank[0:KA, 0:H * TP // 2].bitcast(BF16).rearrange("p (h c u) -> p h c u", h=H, u=U))
                elif kind == "T":
                    b, c = key
                    n = b * NGRP + c // GRP
                    if n >= SLOTS:
                        act.wait_ge(tpos_out[n - SLOTS], 16 * GRP)
                    last = nc.scalar.copy(tpos[:, n % SLOTS * GRP + c % GRP, :], bank[:, 0:TW])
                elif kind == "x":
                    bh, t = divmod(key[0], TILES)
                    if bh >= 2:
                        wait_filled(act, "o", bh - 2)
                    last = nc.scalar.copy(attT[:, bh % 2, :, t * TP:(t + 1) * TP],
                                          bank[0:TP, 0:N].rearrange("p (j n) -> p j n", j=TILES))
                elif kind == "o":
                    b, hh = divmod(key[0], H)
                    last = nc.scalar.copy(oT[b][:, hh, :], bank[0:DV, 0:N])
                elif kind == "f1":
                    b, m = key
                    if b:
                        wait_filled(act, "f2", b - 1, TILES - 1)
                    c = 2 * PAIRS + m
                    last = nc.scalar.activation(hidden[:, m, :], bank[:, 0:N], ACT.Gelu, bias=colv[:, c:c + 1])
                last.then_inc(emptied["A"], 1)

        @block.vector
        def _(dve):
            dve.wait_ge(ld["x0"], 16)
            dve.wait_ge(ld["x1"], 16)
            nc.vector.tensor_reduce(peaks[:, 0:1], early[0:KP, 0:KT * BP], AX_X, ALU.max,
                                    apply_absolute_value=True).then_inc(peak_found, 1)
            dve.wait_ge(ld["w"], 16)
            nc.vector.tensor_reduce(peaks[:, 1:2], early[0:KP, KT * BP:KT * BP + KT * D], AX_X, ALU.max,
                                    apply_absolute_value=True).then_inc(peak_found, 1)
            ln = [0]

            def ln_done(ins):
                ln[0] += 1
                ins.then_inc(ln_step, 1)
                dve.wait_ge(ln_step, ln[0])

            normed = [0]

            def layer_norm(tiles):
                for n in tiles:
                    last = nc.vector.bn_stats(stats[:, n, :], h[:, n, :])
                ln_done(last)
                for n in tiles:
                    last = nc.vector.bn_aggr(meanvar[:, n, :], stats[:, n, :])
                ln_done(last)
                a, z = tiles[0], tiles[-1] + 1
                nc.vector.tensor_scalar(vareps[:, a:z], meanvar[:, a:z, 1], EPS, None, ALU.add).then_inc(var_ready, 1)
                normed[0] += 1
                dve.wait_ge(rstd_ready, normed[0])
                for n in tiles:
                    nc.vector.tensor_scalar(xn[:, n, :], h[:, n, :], meanvar[:, n, 0:1], rstd[:, n:n + 1],
                                            ALU.subtract, ALU.mult).then_inc(xn_ready, 1)

            def reciprocal(g):
                dve.wait_ge(exp_done, g + 1)
                nc.vector.reciprocal(rsum[:, g:g + 1], esum[:, g:g + 1]).then_inc(recip_done, 1)

            for i, (kind, key, eng) in enumerate(items):
                if eng != "V":
                    continue
                bank = psum[:, i % 8, :]
                dve.wait_ge(filled, i + 1)
                if kind == "posg":
                    dve.wait_ge(zeroed, 1)
                    g2 = bank[:, 0:PAIRS * NB].rearrange("p (a f) -> p a f", a=PAIRS)
                    nc.vector.tensor_copy(gpos[0:64, :, 0:NB], g2[0:64])
                    last = nc.vector.tensor_copy(gpos[64:128, :, NB:2 * NB], g2[64:128])
                elif kind == "peak":
                    last = nc.vector.tensor_reduce(srow[:, 0:2], bank[0:1, 0:2 * KP].rearrange("p (a n) -> p a n", a=2),
                                                   AX_X, ALU.max)
                elif kind == "scale":
                    last = nc.vector.tensor_copy(scales[:], bank[0:TP, 0:3])
                elif kind == "tok":
                    b, t = key
                    n, r = b * TILES + t, patches_of(t)
                    if n == 0:
                        dve.wait_ge(ld["rows"], 32)
                    last = nc.vector.scalar_tensor_tensor(out=h[0:r, n, :], in0=bank[0:r, 0:D],
                                                          scalar=scales[0:r, 2:3], in1=tokb[0:r, :],
                                                          op0=ALU.mult, op1=ALU.add)
                elif kind == "q":
                    b, p = key
                    cs = slice(b * N, b * N + N)
                    nc.vector.tensor_scalar(qc[:, p, cs], bank[:, 0:N], DK ** -0.5, colv[:, p:p + 1],
                                            ALU.mult, ALU.add)
                    last = nc.vector.tensor_scalar(qp[:, p, cs], bank[:, 0:N], DK ** -0.5,
                                                   colv[:, PAIRS + p:PAIRS + p + 1], ALU.mult, ALU.add)
                elif kind == "k":
                    b, p = key
                    cs = slice(b * N, b * N + N)
                    nc.vector.tensor_copy(kz[0:64, 2 * p, cs], bank[0:64, 0:N])
                    last = nc.vector.tensor_copy(kz[64:128, 2 * p + 1, cs], bank[64:128, 0:N])
                elif kind == "v":
                    b, t, n = key
                    last = nc.vector.tensor_copy(v[:, b * TILES + t, n * VW:(n + 1) * VW], bank[0:TP, 0:VW])
                elif kind == "a":
                    b = key[0]
                    if b:
                        wait_filled(dve, "aT", b - 1, TILES - 1)
                    dve.wait_ge(zeroed, 2)
                    src = bank[0:TP, 0:TILES * H * NB].rearrange("p (c f) -> p c f", f=NB)
                    a_steps = 3 * b
                    nc.vector.tensor_copy(a3[:, :, 0:NB], src).then_inc(a_step, 1)
                    dve.wait_ge(a_step, a_steps + 1)
                    last = nc.vector.tensor_tensor(arow[:], src, a3[:, :, 0:NB], ALU.subtract)
                elif kind == "aT":
                    b, t = key
                    if b:
                        wait_filled(dve, "T", b - 1, CHUNKS - 1)
                    per = TP // U
                    last = nc.vector.tensor_copy(
                        aT[:, per * t:per * t + per, :].rearrange("p c (u h) -> p h c u", h=H),
                        bank[0:KA, 0:H * TP // 2].bitcast(BF16).rearrange("p (h c u) -> p h c u", h=H, u=U))
                elif kind == "T":
                    b, c = key
                    n = b * NGRP + c // GRP
                    if n >= SLOTS:
                        dve.wait_ge(tpos_out[n - SLOTS], 16 * GRP)
                    last = nc.vector.tensor_copy(tpos[:, n % SLOTS * GRP + c % GRP, :], bank[:, 0:TW])
                elif kind == "s":
                    g = key[0]
                    bh, t = divmod(g, TILES)
                    b, hh = divmod(bh, H)
                    if hh == 0:
                        dve.wait_ge(pos_in[b * TILES + t], 16)
                    last = nc.vector.tensor_tensor_reduce(att_tile(g), bank[0:TP, 0:N], att_tile(g), -1.0, BIG,
                                                          ALU.add, ALU.min, nmax[:, g:g + 1])
                elif kind == "x":
                    bh, t = divmod(key[0], TILES)
                    if bh >= 2:
                        wait_filled(dve, "o", bh - 2)
                    last = nc.vector.tensor_copy(attT[:, bh % 2, :, t * TP:(t + 1) * TP],
                                                 bank[0:TP, 0:N].rearrange("p (j n) -> p j n", j=TILES))
                elif kind == "o":
                    b, hh = divmod(key[0], H)
                    last = nc.vector.tensor_copy(oT[b][:, hh, :], bank[0:DV, 0:N])
                elif kind == "y":
                    n = key[0] * TILES + key[1]
                    dve.wait_ge(bout_added, n + 1)
                    last = nc.vector.tensor_tensor(h[:, n, :], bank[0:TP, 0:D], h[:, n, :], ALU.add)
                elif kind == "f2":
                    n = key[0] * TILES + key[1]
                    wait_filled(dve, "x2T", *key)
                    last = nc.vector.tensor_tensor(xn[:, n, :], bank[0:TP, 0:D], h[:, n, :], ALU.add)
                last.then_inc(emptied["V"], 1)

                if kind == "peak":
                    wait_emptied(dve, "peak")
                    nc.vector.tensor_scalar(srow[:, 2:4], srow[:, 0:2], 1e-8, 1.0 / QMAX, ALU.max,
                                            ALU.mult).then_inc(scale_found, 1)
                    dve.wait_ge(scale_found, 1)
                    nc.vector.tensor_tensor(srow[:, 6:7], srow[:, 2:3], srow[:, 3:4], ALU.mult).then_inc(scale_found, 1)
                    nc.vector.reciprocal(srow[:, 4:6], srow[:, 2:4]).then_inc(scale_found, 1)
                elif kind == "scale":
                    wait_emptied(dve, "scale")
                    pieces = [(wf, 1)] + [(xf[:, :, b * NP:(b + 1) * NP], 0) for b in range(B)]
                    for src, s in pieces:
                        nc.vector.tensor_scalar(src, src, scales[0:KP, s:s + 1], QMAX, ALU.mult,
                                                ALU.min).then_inc(x_scaled, 1)
                    for n, (src, _) in enumerate(pieces):
                        dve.wait_ge(x_scaled, n + 1)
                        nc.vector.tensor_scalar(src, src, -QMAX, ROUND, ALU.max, ALU.add).then_inc(x_shifted, 1)
                elif kind == "tok" and key[1] == TILES - 1:
                    dve.wait_ge(ld["txt"], 16 * B)
                    wait_emptied(dve, "tok", key[0], TILES - 1)
                    layer_norm(range(key[0] * TILES, (key[0] + 1) * TILES))
                elif kind == "a":
                    b = key[0]
                    wait_emptied(dve, "a", b)
                    nc.vector.tensor_copy(a3[:, :, NB:2 * NB], arow[:]).then_inc(a_step, 1)
                    dve.wait_ge(a_step, 3 * b + 2)
                    nc.vector.tensor_tensor(a3[:, :, 2 * NB:3 * NB], arow[:], a3[:, :, NB:2 * NB],
                                            ALU.subtract).then_inc(a_step, 1)
                elif kind == "s" and key[0] >= 1:
                    reciprocal(key[0] - 1)
                    if key[0] == G - 1:
                        reciprocal(G - 1)
                elif kind == "y" and key[1] == TILES - 1:
                    wait_emptied(dve, "y", *key)
                    layer_norm(range(key[0] * TILES, (key[0] + 1) * TILES))

        @block.tensor
        def _(pe):
            for i, (kind, key, eng) in enumerate(items):
                bank = psum[:, i % 8, :]
                if i >= 8:
                    pe.wait_ge(emptied[items[i - 8][2]], emptied_upto[i - 8])
                if kind == "posg":
                    pe.wait_ge(ld["pos"], 32)
                    for p in range(PAIRS):
                        last = nc.tensor.matmul(bank[:, p * NB:(p + 1) * NB], wpos_s[:, p * 128:(p + 1) * 128],
                                                bsum[:], start=True, stop=True)
                elif kind == "peak":
                    pe.wait_ge(peak_found, 2)
                    pe.wait_ge(ld["id"], 16)
                    for n in range(2):
                        last = nc.tensor.matmul(bank[0:1, n * KP:(n + 1) * KP], peaks[:, n:n + 1], idf[0:KP, 0:KP],
                                                start=True, stop=True)
                elif kind == "scale":
                    pe.wait_ge(ones_set, 1)
                    pe.wait_ge(scale_found, 3)
                    last = nc.tensor.matmul(bank[0:TP, 0:3], ones[:], srow[:, 4:7], start=True, stop=True)
                elif kind == "tok":
                    b, t = key
                    r, c0 = patches_of(t), b * NP + t * TP
                    pe.wait_ge(x_rounded, 2 + b)
                    for k in range(KT):
                        last = nc.tensor.matmul(bank[0:r, 0:D], x8[:, k, c0:c0 + r], w8[:, k, :],
                                                start=(k == 0), stop=(k == KT - 1))
                elif kind in ("xnT", "x2T"):
                    b, t = key
                    n = b * TILES + t
                    pe.wait_ge(xn_ready, n + 1 + (B * TILES if kind == "x2T" else 0))
                    for k in range(KT):
                        last = nc.tensor.transpose(bank[0:KP, k * TP:(k + 1) * TP], xn[:, n, k * KP:(k + 1) * KP],
                                                   idf[0:TP, 0:TP])
                elif kind in ("q", "k"):
                    b, p = key
                    w_s = wq_s if kind == "q" else wk_s
                    pe.wait_ge(ld["w" + kind], 16)
                    if kind == "k":
                        pe.wait_ge(zeroed, 6)
                    wait_emptied(pe, "xnT", b, TILES - 1)
                    for k in range(KT):
                        last = nc.tensor.matmul(bank[:, 0:N], w_s[:, k, p * 128:(p + 1) * 128],
                                                xnT[:, k, b * N:b * N + N], start=(k == 0), stop=(k == KT - 1))
                elif kind == "v":
                    b, t, n = key
                    pe.wait_ge(ld["wv"], 16)
                    c0 = b * N + t * TP
                    for k in range(KT):
                        last = nc.tensor.matmul(bank[0:TP, 0:VW], xnT[:, k, c0:c0 + TP],
                                                wv_s[:, k, n * VW:(n + 1) * VW], start=(k == 0), stop=(k == KT - 1))
                elif kind == "a":
                    b = key[0]
                    wait_emptied(pe, "posg")
                    for p in range(PAIRS):
                        wait_emptied(pe, "q", b, p)
                    for t in range(TILES):
                        for p in range(PAIRS):
                            c0, o0 = b * N + t * TP, t * H * NB + p * 2 * NB
                            last = nc.tensor.matmul(bank[0:TP, o0:o0 + 2 * NB], qp[:, p, c0:c0 + TP], gpos[:, p, :],
                                                    start=True, stop=True)
                elif kind == "aT":
                    b, t = key
                    pe.wait_ge(id_cast, 1)
                    pe.wait_ge(a_step, 3 * b + 3)
                    bb = bank[0:KA, 0:H * TP // 2].bitcast(BF16)
                    for hh in range(H):
                        last = nc.tensor.transpose(bb[:, hh * TP:(hh + 1) * TP], a3[:, t * H + hh, :], idb[:])
                elif kind == "T":
                    b, c = key
                    pe.wait_ge(mask_cast, 1)
                    wait_emptied(pe, "aT", b, c // (TP // U))
                    first = N - 1 - (U * c + U - 1)
                    last = nc.tensor.matmul(bank[:, 0:TW], aT[:, c, :], mask[:, first:first + TW],
                                            start=True, stop=True)
                elif kind == "s":
                    bh, t = divmod(key[0], TILES)
                    b, hh = divmod(bh, H)
                    wait_emptied(pe, "q", b, hh // 2)
                    wait_emptied(pe, "k", b, hh // 2)
                    c0 = b * N + t * TP
                    last = nc.tensor.matmul(bank[0:TP, 0:N], qc[:, hh // 2, c0:c0 + TP], kz[:, hh, b * N:b * N + N],
                                            start=True, stop=True)
                elif kind == "x":
                    g = key[0]
                    pe.wait_ge(weights_done, g + 1)
                    e = att_tile(g)
                    for j in range(TILES):
                        last = nc.tensor.transpose(bank[0:TP, j * TP:(j + 1) * TP], e[:, j * TP:(j + 1) * TP],
                                                   idf[0:TP, 0:TP])
                elif kind == "o":
                    bh = key[0]
                    b, hh = divmod(bh, H)
                    for t in range(TILES):
                        wait_emptied(pe, "x", bh * TILES + t)
                        for n in range(VH):
                            wait_emptied(pe, "v", b, t, n)
                    for j in range(TILES):
                        last = nc.tensor.matmul(bank[0:DV, 0:N], v[:, b * TILES + j, hh * DV:(hh + 1) * DV],
                                                attT[:, bh % 2, j, :], start=(j == 0), stop=(j == TILES - 1))
                elif kind == "y":
                    b, t = key
                    pe.wait_ge(ld["wo"], 16)
                    for hh in range(H):
                        wait_emptied(pe, "o", b * H + hh)
                    for hh in range(H):
                        last = nc.tensor.matmul(bank[0:TP, 0:D], oT[b][:, hh, t * TP:(t + 1) * TP], wo_s[:, hh, :],
                                                start=(hh == 0), stop=(hh == H - 1))
                elif kind == "f1":
                    b, m = key
                    pe.wait_ge(ld["w1"], 16)
                    wait_emptied(pe, "x2T", b, TILES - 1)
                    for k in range(KT):
                        last = nc.tensor.matmul(bank[:, 0:N], w1_s[:, k, m * 128:(m + 1) * 128],
                                                xnT[:, k, b * N:b * N + N], start=(k == 0), stop=(k == KT - 1))
                elif kind == "f2":
                    b, t = key
                    pe.wait_ge(ld["w2"], 16)
                    wait_emptied(pe, "f1", b, HID - 1)
                    for m in range(HID):
                        last = nc.tensor.matmul(bank[0:TP, 0:D], hidden[:, m, t * TP:(t + 1) * TP], w2_s[:, m, :],
                                                start=(m == 0), stop=(m == HID - 1))
                last.then_inc(filled, 1)


def kernel(x, txt, L0_tok_w, L0_tok_b, L0_attn_Wq, L0_attn_Wk, L0_attn_Wv, L0_attn_Wout, L0_attn_bout,
           L0_attn_Wpos, L0_attn_rel_content_bias, L0_attn_rel_pos_bias, L0_ffn_in_weight, L0_ffn_in_bias,
           L0_ffn_out_weight):
    import numpy as np
    import concourse.bacc as bacc
    from concourse import mybir as my
    from concourse.bass_utils import run_bass_kernel_spmd

    def a(v):
        return np.asarray(v)

    def chunks(m, size):
        return m.reshape(m.shape[0] // size, size, m.shape[1]).transpose(1, 0, 2)

    B, C, HH, WW = x.shape
    D, _, P, _ = L0_tok_w.shape
    gh, gw = HH // P, WW // P
    F = L0_attn_Wpos.shape[0]
    HIDDEN = L0_ffn_in_weight.shape[0]
    N = gh * gw + txt.shape[1]
    KP = 96
    H = L0_attn_rel_content_bias.shape[1]

    patches = a(x).reshape(B, C, gh, P, gw, P).transpose(1, 3, 5, 0, 2, 4).reshape(C * P * P, B * gh * gw)
    wpat = a(L0_tok_w).reshape(D, C * P * P).transpose(1, 0)
    cols = np.concatenate([
        a(L0_attn_rel_content_bias).reshape(-1, 128).transpose(1, 0),
        a(L0_attn_rel_pos_bias).reshape(-1, 128).transpose(1, 0),
        a(L0_ffn_in_bias).reshape(-1, 128).transpose(1, 0)], axis=1)
    narrow = [f for f in range(1, F + 1) if 2 ** f - 1 < N]
    nb = len(narrow) + 1
    bucket_sum = np.zeros((F, nb), np.float32)
    for f in range(1, F + 1):
        bucket_sum[f - 1, min(f, nb) - 1] = 1.0
    rel = np.abs(np.arange(-(N - 1), N))
    bucket_mask = np.zeros((3, nb, 2 * N - 1), np.float32)
    for f in range(1, nb + 1):
        bucket_mask[:, f - 1, :] = np.where(rel < 2 ** f - 1, 1.0, 0.0)
    ins = {
        "xpat": chunks(patches, KP), "txt": a(txt), "wpat": chunks(wpat, KP), "tok_b": a(L0_tok_b),
        "wq": chunks(a(L0_attn_Wq), KP), "wk": chunks(a(L0_attn_Wk), KP), "wv": chunks(a(L0_attn_Wv), KP),
        "wout": chunks(a(L0_attn_Wout), L0_attn_Wout.shape[0] // H), "bout": a(L0_attn_bout),
        "wpos": a(L0_attn_Wpos), "cols": cols,
        "w1": chunks(a(L0_ffn_in_weight).transpose(1, 0), KP), "w2": chunks(a(L0_ffn_out_weight), 128),
        "ident": np.eye(128, dtype=np.float32), "bucket_sum": bucket_sum,
        "bucket_mask": bucket_mask.reshape(3 * nb, 2 * N - 1),
    }
    nc = bacc.Bacc("TRN2", target_bir_lowering=False, num_devices=1)
    arrays, args = {}, []
    for name, arr in ins.items():
        arr = np.ascontiguousarray(arr)
        arrays["in_" + name] = arr
        args.append(nc.dram_tensor("in_" + name, arr.shape, my.dt.from_np(arr.dtype), kind="ExternalInput").ap())
    out = nc.dram_tensor("out_h", (B, N, D), my.dt.float32, kind="ExternalOutput").ap()
    early_fusion_kernel(nc, *args, out)
    r = run_bass_kernel_spmd(nc, [arrays], core_ids=[0])
    return r.results[0]["out_h"]
```

```python
from contextlib import ExitStack

import concourse.bass as bass
from concourse import mybir

F32 = mybir.dt.float32
BF16 = mybir.dt.bfloat16
ALU = mybir.AluOpType
ACT = mybir.ActivationFunctionType
AX_X = mybir.AxisListType.X

QMAX = 127.0
ROUND = 1.5 * 2.0 ** 23
BIG = 3.0e38
EPS = 1e-5
WARM = {("peak",): 9, ("scale",): 3, ("tok", 1): 10, ("xnT", 0): 12}


def attention_tiles(H):
    tiles = []
    for g in range(H // 4):
        tiles.append((2, g))
        for h in range(4 * g, 4 * g + 4):
            tiles += [(0, h), (1, h)]
    return tiles


def plan_items(B, H, PAIRS, CHUNKS, HID, VH, LAG):
    items = []
    turn = [0]

    def add(kind, *key, eng=None):
        if eng is None:
            eng = "AV"[turn[0] % 2]
            turn[0] += 1
        items.append((kind, key, eng))

    tiles = attention_tiles(H)
    per = len(tiles)
    chunks = list(range(CHUNKS - 2, CHUNKS)) + list(range(CHUNKS - 2))

    add("peak", eng="V")
    add("scale", eng="V")
    for n in range(1, 1 + 2 * B):
        add("tok", n, eng="V")
    add("posg", eng="V")
    for n in range(3):
        add("xnT", n, eng="A")
    for p in range(PAIRS):
        add("q", 0, p)
    for n in range(3, 1 + 2 * B):
        add("xnT", n, eng="A")
    add("k", 0, 0)
    add("a", 0, eng="V")
    for p in range(1, PAIRS):
        add("k", 0, p)
    big = [("q", 1, p) for p in range(PAIRS)] + [("k", 1, p) for p in range(PAIRS)]
    big += [("v", n, half) for n in range(3) for half in range(VH)]
    for t in (2, 0, 1):
        add("aT", 0, t)
    for n, c in enumerate(chunks):
        add("T", 0, c)
        if n % 3 != 2 and big:
            add(*big.pop(0))
    for it in big[:2]:
        add(*it)
    add("a", 1, eng="V")
    rest = big[2:] + [("v", n, half) for n in range(3, 1 + 2 * B) for half in range(VH)]
    for it in rest[:3]:
        add(*it)
    for n, t in enumerate((2, 0, 1)):
        add("aT", 1, t)
    waiting = [("T", 1, c) for c in chunks]
    for it in rest[3:]:
        add(*it)
        add(*waiting.pop(0))

    G = B * per
    early = {per + LAG + 5: ("y", 1), per + LAG + 7: ("y", 2), G + LAG - 3: ("x2T", 1), G + LAG - 2: ("x2T", 2)}
    engines = {"y": "V", "x2T": "A", "f1": "A", "f2": "V"}
    ready = []
    for g in range(G + LAG):
        if g < G:
            add("s", g, eng="V")
        if waiting:
            add(*waiting.pop(0))
        if g >= LAG:
            add("x", g - LAG)
            if ready and ready[0][0] <= g - 2:
                add("o", ready.pop(0)[1])
            b, n = divmod(g - LAG, per)
            t, h = tiles[n]
            if t == 1:
                ready.append((g, b * H + h))
        if g in early:
            add(*early[g], eng=engines[early[g][0]])
    f1 = [("f1", 0, m) for m in range(HID)]
    tail = f1[:1] + [("o", head) for _, head in ready] + f1[1:3] + [("y", 3), ("y", 4), ("y", 0)] + f1[3:]
    tail += [("f2", 1), ("x2T", 3), ("x2T", 4), ("x2T", 0), ("f2", 2)]
    tail += [("f1", group, m) for group in (1, 2) for m in range(HID)] + [("f2", 3), ("f2", 4), ("f2", 0)]
    for it in tail:
        add(*it, eng=engines.get(it[0]))
    return items


def early_fusion_kernel(nc, xpat, txt, wpat, tok_b, wq, wk, wv, wout, bout, wpos, cols, w1, w2,
                        ident, bucket_sum, bucket_mask, out):
    KP, KT, BP = xpat.shape
    B, NT, D = txt.shape
    NP = BP // B
    N = NP + NT
    TP = 128
    NTILES = 1 + 2 * B
    HDK = wq.shape[2]
    PAIRS = HDK // 128
    DK = 64
    H = HDK // DK
    HDV = wv.shape[2]
    DV = HDV // H
    HID = w1.shape[2] // 128
    F = wpos.shape[0]
    NB = bucket_sum.shape[1]
    REL = 2 * N - 1
    SPLIT = 3
    KA = 96
    U = 16
    CHUNKS = N // U
    TW = N + U - 1
    PITCH = 2 * N
    GRP = 2
    NGRP = CHUNKS // GRP
    SLOTS = 3
    VH = 2
    VW = HDV // VH
    LAG = 4
    RING = 5
    JT = 3
    tiles = attention_tiles(H)
    PER = len(tiles)
    G = B * PER
    ATILE = (0, TP, N - TP)
    assert NP == 2 * TP and NT == 32 and U * H == 128 and SPLIT * NB <= KA and H % 4 == 0 and B == 2

    items = plan_items(B, H, PAIRS, CHUNKS, HID, VH, LAG)
    index = {(kind, *key): i for i, (kind, key, _) in enumerate(items)}
    order = [key[1] for kind, key, _ in items if kind == "T" and key[0] == 0]
    group_of = {c: n // GRP for n, c in enumerate(order)}

    with ExitStack() as ctx:
        def sb(name, shape, dt=F32):
            return ctx.enter_context(nc.sbuf_tensor(name, shape, dt))

        def sem(name):
            return ctx.enter_context(nc.semaphore(name))

        psum = ctx.enter_context(nc.psum_tensor("psum", [128, 8, 512], F32))
        skew = [nc.dram_tensor(f"skew{b}", [H, N, PITCH], F32, kind="Internal") for b in range(B)]

        early = sb("early", [128, max(KT * BP + KT * D, HID * NP)])
        xf = early[0:KP, 0:KT * BP].rearrange("p (k n) -> p k n", k=KT)
        wf = early[0:KP, KT * BP:KT * BP + KT * D].rearrange("p (k n) -> p k n", k=KT)
        idf = sb("idf", [128, 128])
        idb = sb("idb", [128, 128], BF16)
        warm = sb("warm", [128, 512], BF16)
        ones = sb("ones", [1, TP])
        peaks = sb("peaks", [KP, 3])
        srow = sb("srow", [1, 8])
        scales = sb("scales", [TP, 3])
        tokb = sb("tokb", [TP, D])
        boutb = sb("boutb", [TP, D])
        colv = sb("colv", [128, cols.shape[1]])
        wq_s = sb("wq_s", [KP, KT, HDK])
        wk_s = sb("wk_s", [KP, KT, HDK])
        wv_s = sb("wv_s", [KP, KT, HDV])
        wo_s = sb("wo_s", [DV, H, D])
        w1_s = sb("w1_s", [KP, KT, HID * 128])
        w2_s = sb("w2_s", [128, HID, D])
        wpos_s = sb("wpos_s", [F, HDK])
        bsum = sb("bsum", [F, NB])
        mask = sb("mask", [KA, REL + 1], BF16)
        gpos = sb("gpos", [128, PAIRS, 2 * NB])
        h = sb("h", [TP, NTILES, D])
        xn = sb("xn", [TP, NTILES, D])
        stats = sb("stats", [TP, NTILES, 6])
        meanvar = sb("meanvar", [TP, NTILES, 2])
        vareps = sb("vareps", [TP, NTILES])
        neghalf = sb("neghalf", [TP, NTILES])
        rstd = sb("rstd", [TP, NTILES])
        xnT = sb("xnT", [KP, KT, B * N])
        qc = sb("qc", [128, PAIRS, B * N])
        qp = sb("qp", [128, PAIRS, B * N])
        kz = sb("kz", [128, H, B * N])
        v = sb("v", [TP, B * JT, HDV])
        arow = sb("arow", [TP, JT * H, NB])
        a3 = sb("a3", [TP, JT * H, KA], BF16)
        aT = sb("aT", [KA, CHUNKS, 128], BF16)
        tpos = sb("tpos", [128, SLOTS * GRP, TW])
        att = sb("att", [TP, B, PER, JT * TP])
        nmax = sb("nmax", [TP, G])
        esum = sb("esum", [TP, G])
        rsum = sb("rsum", [TP, G])
        attT = sb("attT", [TP, RING, JT, N])
        oT1 = sb("oT1", [DV, H, N])
        oT = [qp[0:DV, :, :].rearrange("p a n -> p (a n)")[:, 0:H * N].rearrange("p (h n) -> p h n", h=H), oT1]
        attT_flat = attT[:].rearrange("p r j n -> p (r j n)")
        x8 = attT_flat[0:KP, 0:KT * BP // 2].bitcast(BF16).rearrange("p (k n) -> p k n", k=KT)
        w8 = attT_flat[0:KP, KT * BP // 2:KT * (BP + D) // 2].bitcast(BF16).rearrange("p (k n) -> p k n", k=KT)
        maskf = attT_flat[0:SPLIT * NB, KT * (BP + D) // 2:KT * (BP + D) // 2 + REL]
        qc_flat = qc[:].rearrange("p a n -> p (a n)")
        hidden = [early[:, 0:HID * NP].rearrange("p (m n) -> p m n", m=HID),
                  qc_flat[:, 0:HID * NP].rearrange("p (m n) -> p m n", m=HID),
                  qc_flat[:, HID * NP:HID * (NP + B * NT)].rearrange("p (m n) -> p m n", m=HID)]

        filled = sem("filled")
        emptied = {"A": sem("emptied_by_act"), "V": sem("emptied_by_dve")}
        ld = {n: sem("ld_" + n) for n in ("x0", "x1", "w", "id", "rows", "txt", "cols", "pos", "mask", "wq", "wk",
                                          "wv", "wo", "w1", "w2")}
        peak_found = sem("peak_found")
        scale_found = sem("scale_found")
        x_scaled = sem("x_scaled")
        x_shifted = sem("x_shifted")
        x_rounded = sem("x_rounded")
        warm_set = sem("warm_set")
        zeroed = sem("zeroed")
        kz_half = sem("kz_half")
        id_cast = sem("id_cast")
        mask_cast = sem("mask_cast")
        ones_set = sem("ones_set")
        ln_step = sem("ln_step")
        var_ready = sem("var_ready")
        rstd_ready = sem("rstd_ready")
        xn_ready = sem("xn_ready")
        bout_added = sem("bout_added")
        a_step = sem("a_step")
        tpos_out = [sem(f"tpos_out{i}") for i in range(B * NGRP)]
        pos_in = [sem(f"pos_in{i}") for i in range(B * 3)]
        exp_done = sem("exp_done")
        recip_done = sem("recip_done")
        weights_done = sem("weights_done")
        out_done = sem("out_done")

        zero_order = ["gpos", "h", "a3", "mask", "kz", "v", "att0", "att1"]
        norm_order = [(1, n) for n in range(NTILES)] + [(2, n) for n in (1, 2, 3, 4, 0)]
        root_ranges = [(0, 3), (3, NTILES), (1, 3), (0, NTILES)]

        emptied_upto = []
        count = {"A": 0, "V": 0}
        for _, _, e in items:
            count[e] += 1
            emptied_upto.append(count[e])

        def wait_filled(eng, *key):
            eng.wait_ge(filled, index[key] + 1)

        def wait_emptied(eng, *key):
            i = index[key]
            eng.wait_ge(emptied[items[i][2]], emptied_upto[i])

        def wait_zeroed(eng, what):
            eng.wait_ge(zeroed, zero_order.index(what) + 1)

        def wait_normed(eng, which, n):
            eng.wait_ge(xn_ready, norm_order.index((which, n)) + 1)

        def att_tile(g):
            b, n = divmod(g, PER)
            t, hh = tiles[n]
            return att[:, b, t * H + hh, :]

        def cols_of(tile):
            if tile == 0:
                return xnT[:].rearrange("p k (b n) -> p k b n", b=B)[:, :, :, NP:N]
            c0 = (tile - 1) // 2 * N + (tile - 1) % 2 * TP
            return xnT[:, :, c0:c0 + TP]

        def empty_weights(copy, eng, g, bank):
            b, n = divmod(g, PER)
            t, hh = tiles[n]
            src = bank[:, 0:JT * TP].rearrange("p (j n) -> p j n", j=JT)
            last_head = b * H + (hh if t < 2 else 4 * hh + 3)
            if last_head >= RING:
                wait_filled(eng, "o", last_head - RING)
            if t < 2:
                return copy(attT[:, last_head % RING, :, t * TP:(t + 1) * TP], src)
            src = src.rearrange("p j (h n) -> p h j n", h=4)
            r0 = (b * H + 4 * hh) % RING
            k = min(4, RING - r0)
            done = copy(attT[:, r0:r0 + k, :, NP:N], src[:, 0:k])
            if k < 4:
                done = copy(attT[:, 0:4 - k, :, NP:N], src[:, k:4])
            return done

        def empty_bands(copy, eng, b, t, bank):
            if b:
                wait_filled(eng, "T", b - 1, order[-1])
            src = bank[0:KA, :].bitcast(BF16).rearrange("p (h c u) -> p h c u", h=H, u=U)
            per = TP // U
            c0, skip = (t * per, 0) if t < 2 else (2 * per, per - NT // U)
            dst = aT[:, c0:c0 + per - skip, :].rearrange("p c (u h) -> p h c u", h=H)
            return copy(dst, src[:, :, skip:per, :])

        def empty_tpos(copy, eng, b, c, bank):
            n = b * NGRP + group_of[c]
            if n >= SLOTS:
                eng.wait_ge(tpos_out[n - SLOTS], 16 * GRP)
            return copy(tpos[:, n % SLOTS * GRP + order.index(c) % GRP, :], bank[:, 0:TW])

        def empty_v(copy, eng, n, half, bank):
            vs = slice(half * VW, (half + 1) * VW)
            if n == 0:
                wait_zeroed(eng, "v")
                for b in range(B):
                    done = copy(v[0:NT, b * JT + 2, vs], bank[b * NT:(b + 1) * NT, 0:VW])
                return done
            return copy(v[:, (n - 1) // 2 * JT + (n - 1) % 2, vs], bank[:, 0:VW])

        LN_AT = sum(kind == "s" for kind, _, _ in items[:index["y", 2]])

        ctx.enter_context(nc.allow_non_contiguous_dma(reason="rows of a few hundred bytes"))
        block = ctx.enter_context(nc.Block())

        @block.sync
        def _(sp):
            sp.dma_start(xf[:, 0, :], xpat[:, 0, :]).then_inc(ld["x0"], 16)
            sp.dma_start(wf, wpat).then_inc(ld["w"], 16)
            sp.dma_start(wq_s[:], wq).then_inc(ld["wq"], 16)
            sp.dma_start(wk_s[:], wk).then_inc(ld["wk"], 16)
            sp.dma_start(wv_s[:], wv).then_inc(ld["wv"], 16)
            sp.dma_start(wo_s[:], wout).then_inc(ld["wo"], 16)
            sp.dma_start(w1_s[:], w1).then_inc(ld["w1"], 16)
            sp.dma_start(w2_s[:], w2).then_inc(ld["w2"], 16)

            def send(b, grp):
                chunks = order[GRP * grp:GRP * grp + GRP]
                for c in chunks:
                    wait_emptied(sp, "T", b, c)
                slot = (b * NGRP + grp) % SLOTS
                for n, c in enumerate(chunks):
                    first = N - 1 - (U * c + U - 1)
                    dst = bass.AP(skew[b], U * c * PITCH + first, [[PITCH, U], [N * PITCH, H], [1, TW]])
                    sp.dma_start(dst, tpos[:, slot * GRP + n, :]).then_inc(tpos_out[b * NGRP + grp], 16)

            def fetch(b, t):
                for c in range(t * TP // U, min(CHUNKS, (t + 1) * TP // U)):
                    sp.wait_ge(tpos_out[b * NGRP + group_of[c]], 16 * GRP)
                start = t * TP * PITCH + N - 1 - t * TP
                if t < 2:
                    src = bass.AP(skew[b], start, [[PITCH - 1, TP], [N * PITCH, H], [1, N]])
                    sp.dma_start(att[:, b, t * H:(t + 1) * H, 0:N], src).then_inc(pos_in[b * 3 + t], 16)
                    return
                for q in range(4):
                    src = bass.AP(skew[b], start + q * N * PITCH, [[PITCH - 1, NT], [4 * N * PITCH, H // 4], [1, N]])
                    sp.dma_start(att[q * NT:(q + 1) * NT, b, 2 * H:2 * H + H // 4, 0:N],
                                 src).then_inc(pos_in[b * 3 + 2], 16)

            for b in range(B):
                for grp in range(NGRP):
                    send(b, grp)
                    if grp == 1:
                        fetch(b, 2)
                    if grp == 5:
                        fetch(b, 0)
                fetch(b, 1)
            for n in (1, 2, 3, 4, 0):
                wait_emptied(sp, "f2", n)
                if n:
                    b, t = divmod(n - 1, 2)
                    sp.dma_start(out[b, t * TP:(t + 1) * TP, :], xn[:, n, :]).then_inc(out_done, 16)
                else:
                    for b in range(B):
                        sp.dma_start(out[b, NP:N, :], xn[b * NT:(b + 1) * NT, 0, :]).then_inc(out_done, 16)
            sp.wait_ge(out_done, 16 * (NTILES - 1 + B))

        @block.gpsimd
        def _(pool):
            nc.gpsimd.memset(ones[:], 1.0).then_inc(ones_set, 1)
            nc.gpsimd.memset(neghalf[:], -0.5).then_inc(ones_set, 1)
            nc.gpsimd.memset(gpos[:], 0.0).then_inc(zeroed, 1)
            pool.wait_ge(zeroed, 1)
            nc.gpsimd.memset(h[B * NT:TP, 0, :], 0.0).then_inc(zeroed, 1)
            pool.wait_ge(zeroed, 2)
            nc.gpsimd.memset(a3[:, :, SPLIT * NB:KA], 0.0).then_inc(zeroed, 1)
            nc.gpsimd.memset(mask[:], 0.0).then_inc(zeroed, 1)
            pool.wait_ge(ld["id"], 16)
            nc.gpsimd.tensor_copy(idb[:], idf[:]).then_inc(id_cast, 1)
            pool.wait_ge(id_cast, 1)
            kz2 = kz[:].rearrange("p (a two) n -> p a two n", two=2)
            nc.gpsimd.memset(kz2[0:64, :, 1, :], 0.0).then_inc(kz_half, 1)
            pool.wait_ge(kz_half, 1)
            nc.gpsimd.memset(kz2[64:128, :, 0, :], 0.0).then_inc(zeroed, 1)
            pool.wait_ge(ld["mask"], 16)
            pool.wait_ge(zeroed, 5)
            nc.gpsimd.tensor_copy(mask[0:SPLIT * NB, 0:REL], maskf).then_inc(mask_cast, 1)

            def root(nth):
                pool.wait_ge(var_ready, nth + 1)
                a, z = root_ranges[nth]
                nc.gpsimd.tensor_tensor(rstd[:, a:z], vareps[:, a:z], neghalf[:, a:z],
                                        ALU.pow).then_inc(rstd_ready, 1)

            pool.wait_ge(ones_set, 2)
            root(0)
            root(1)
            nc.gpsimd.memset(v[:].rearrange("p (b j) n -> p b j n", j=JT)[:, :, 2, :], 0.0).then_inc(zeroed, 1)
            for b in range(B):
                nc.gpsimd.memset(att[:, b, :, N:JT * TP], 0.0).then_inc(zeroed, 1)
            for n in range(NTILES):
                wait_normed(pool, 1, n)
                nc.gpsimd.tensor_tensor(h[:, n, :], h[:, n, :], boutb[:], ALU.add).then_inc(bout_added, 1)
            for g in range(G):
                if g == LN_AT:
                    root(2)
                pool.wait_ge(recip_done, g + 1)
                e = att_tile(g)[:, 0:N]
                nc.gpsimd.tensor_scalar(e, e, rsum[:, g:g + 1], 1.0, ALU.mult, ALU.mult).then_inc(weights_done, 1)
            root(3)

        @block.scalar
        def _(act):
            act.dma_start(xf[:, 1, :], xpat[:, 1, :]).then_inc(ld["x1"], 16)
            act.dma_start(idf[:], ident).then_inc(ld["id"], 16)
            act.dma_start(tokb[:], tok_b.partition_broadcast(TP)).then_inc(ld["rows"], 16)
            act.dma_start(boutb[:], bout.partition_broadcast(TP)).then_inc(ld["rows"], 16)
            act.dma_start(h[0:B * NT, 0, :], txt.rearrange("b n d -> (b n) d")).then_inc(ld["txt"], 16)
            act.dma_start(wpos_s[:], wpos).then_inc(ld["pos"], 16)
            act.dma_start(bsum[:], bucket_sum).then_inc(ld["pos"], 16)
            act.dma_start(colv[:], cols).then_inc(ld["cols"], 16)
            act.dma_start(maskf, bucket_mask).then_inc(ld["mask"], 16)

            act.wait_ge(x_shifted, 1)
            nc.scalar.activation(w8, wf, ACT.Copy, bias=-ROUND).then_inc(x_rounded, 1)
            for b in range(B):
                act.wait_ge(x_shifted, 2 + b)
                nc.scalar.activation(x8[:, :, b * NP:(b + 1) * NP], xf[:, :, b * NP:(b + 1) * NP], ACT.Copy,
                                     bias=-ROUND).then_inc(x_rounded, 1)
            act.wait_ge(ld["cols"], 16)

            for i, (kind, key, eng) in enumerate(items):
                bank = psum[:, i % 8, :]
                if kind == "s":
                    g = key[0]
                    wait_emptied(act, "s", g)
                    e = att_tile(g)[:, 0:N]
                    nc.scalar.activation(e, e, ACT.Exp, bias=nmax[:, g:g + 1], scale=-1.0,
                                         accum_out=esum[:, g:g + 1]).then_inc(exp_done, 1)
                if eng != "A":
                    continue
                act.wait_ge(filled, i + 1)
                if kind in ("xnT", "x2T"):
                    src = bank[0:KP, 0:KT * TP].rearrange("p (k n) -> p k n", k=KT)
                    if key[0] == 0:
                        src = src[:, :, 0:B * NT].rearrange("p k (b n) -> p k b n", b=B)
                    last = nc.scalar.copy(cols_of(key[0]), src)
                elif kind == "q":
                    b, p = key
                    cs = slice(b * N, b * N + N)
                    nc.scalar.activation(qc[:, p, cs], bank[:, 0:N], ACT.Identity, bias=colv[:, p:p + 1],
                                         scale=DK ** -0.5)
                    last = nc.scalar.activation(qp[:, p, cs], bank[:, 0:N], ACT.Identity,
                                                bias=colv[:, PAIRS + p:PAIRS + p + 1], scale=DK ** -0.5)
                elif kind == "k":
                    b, p = key
                    cs = slice(b * N, b * N + N)
                    nc.scalar.copy(kz[0:64, 2 * p, cs], bank[0:64, 0:N])
                    last = nc.scalar.copy(kz[64:128, 2 * p + 1, cs], bank[64:128, 0:N])
                elif kind == "v":
                    last = empty_v(nc.scalar.copy, act, *key, bank)
                elif kind == "aT":
                    last = empty_bands(nc.scalar.copy, act, *key, bank)
                elif kind == "T":
                    last = empty_tpos(nc.scalar.copy, act, *key, bank)
                elif kind == "x":
                    last = empty_weights(nc.scalar.copy, act, key[0], bank)
                elif kind == "o":
                    b, hh = divmod(key[0], H)
                    last = nc.scalar.copy(oT[b][:, hh, :], bank[0:DV, 0:N])
                elif kind == "f1":
                    group, m = key
                    c = 2 * PAIRS + m
                    last = nc.scalar.activation(hidden[group][:, m, :], bank[:, 0:hidden[group].shape[2]], ACT.Gelu,
                                                bias=colv[:, c:c + 1])
                last.then_inc(emptied["A"], 1)

        @block.vector
        def _(dve):
            nc.vector.memset(warm[:], 0.0).then_inc(warm_set, 1)
            for k in range(KT):
                dve.wait_ge(ld[f"x{k}"], 16)
                nc.vector.tensor_reduce(peaks[:, k:k + 1], xf[:, k, :], AX_X, ALU.max,
                                        apply_absolute_value=True).then_inc(peak_found, 1)
            dve.wait_ge(ld["w"], 16)
            nc.vector.tensor_reduce(peaks[:, KT:KT + 1], early[0:KP, KT * BP:KT * BP + KT * D], AX_X, ALU.max,
                                    apply_absolute_value=True).then_inc(peak_found, 1)
            ln = [0]

            def ln_done(ins):
                ln[0] += 1
                ins.then_inc(ln_step, 1)
                dve.wait_ge(ln_step, ln[0])

            def moments(nth, group):
                for n in group:
                    last = nc.vector.bn_stats(stats[:, n, :], h[:, n, :])
                ln_done(last)
                for n in group:
                    last = nc.vector.bn_aggr(meanvar[:, n, :], stats[:, n, :])
                ln_done(last)
                a, z = root_ranges[nth]
                nc.vector.tensor_scalar(vareps[:, a:z], meanvar[:, a:z, 1], EPS, None, ALU.add).then_inc(var_ready, 1)

            def normalise(nth, group):
                dve.wait_ge(rstd_ready, nth + 1)
                for n in group:
                    nc.vector.tensor_scalar(xn[:, n, :], h[:, n, :], meanvar[:, n, 0:1], rstd[:, n:n + 1],
                                            ALU.subtract, ALU.mult).then_inc(xn_ready, 1)

            def reciprocal(g):
                dve.wait_ge(exp_done, g + 1)
                nc.vector.reciprocal(rsum[:, g:g + 1], esum[:, g:g + 1]).then_inc(recip_done, 1)

            for i, (kind, key, eng) in enumerate(items):
                if eng != "V":
                    continue
                bank = psum[:, i % 8, :]
                dve.wait_ge(filled, i + 1)
                if kind == "posg":
                    wait_zeroed(dve, "gpos")
                    g2 = bank[:, 0:PAIRS * NB].rearrange("p (a f) -> p a f", a=PAIRS)
                    nc.vector.tensor_copy(gpos[0:64, :, 0:NB], g2[0:64])
                    last = nc.vector.tensor_copy(gpos[64:128, :, NB:2 * NB], g2[64:128])
                elif kind == "peak":
                    nc.vector.tensor_reduce(srow[:, 0:1], bank[0:1, 0:KT * KP], AX_X, ALU.max)
                    last = nc.vector.tensor_reduce(srow[:, 1:2], bank[0:1, KT * KP:(KT + 1) * KP], AX_X, ALU.max)
                elif kind == "scale":
                    last = nc.vector.tensor_copy(scales[:], bank[:, 0:3])
                elif kind == "tok":
                    n = key[0]
                    if n == 1:
                        dve.wait_ge(ld["rows"], 32)
                    last = nc.vector.scalar_tensor_tensor(out=h[:, n, :], in0=bank[:, 0:D], scalar=scales[:, 2:3],
                                                          in1=tokb[:], op0=ALU.mult, op1=ALU.add)
                elif kind == "q":
                    b, p = key
                    cs = slice(b * N, b * N + N)
                    nc.vector.tensor_scalar(qc[:, p, cs], bank[:, 0:N], DK ** -0.5, colv[:, p:p + 1],
                                            ALU.mult, ALU.add)
                    last = nc.vector.tensor_scalar(qp[:, p, cs], bank[:, 0:N], DK ** -0.5,
                                                   colv[:, PAIRS + p:PAIRS + p + 1], ALU.mult, ALU.add)
                elif kind == "k":
                    b, p = key
                    cs = slice(b * N, b * N + N)
                    nc.vector.tensor_copy(kz[0:64, 2 * p, cs], bank[0:64, 0:N])
                    last = nc.vector.tensor_copy(kz[64:128, 2 * p + 1, cs], bank[64:128, 0:N])
                elif kind == "v":
                    last = empty_v(nc.vector.tensor_copy, dve, *key, bank)
                elif kind == "a":
                    b = key[0]
                    if b:
                        wait_filled(dve, "aT", b - 1, 1)
                    src = bank[:, 0:JT * H * NB].rearrange("p (c f) -> p c f", f=NB)
                    nc.vector.tensor_copy(a3[:, :, 0:NB], src).then_inc(a_step, 1)
                    dve.wait_ge(a_step, 3 * b + 1)
                    last = nc.vector.tensor_tensor(arow[:], src, a3[:, :, 0:NB], ALU.subtract)
                elif kind == "aT":
                    last = empty_bands(nc.vector.tensor_copy, dve, *key, bank)
                elif kind == "T":
                    last = empty_tpos(nc.vector.tensor_copy, dve, *key, bank)
                elif kind == "s":
                    g = key[0]
                    b, n = divmod(g, PER)
                    dve.wait_ge(pos_in[b * 3 + tiles[n][0]], 16 * (4 if tiles[n][0] == 2 else 1))
                    e = att_tile(g)[:, 0:N]
                    last = nc.vector.tensor_tensor_reduce(e, bank[:, 0:N], e, -1.0, BIG, ALU.add, ALU.min,
                                                          nmax[:, g:g + 1])
                elif kind == "x":
                    last = empty_weights(nc.vector.tensor_copy, dve, key[0], bank)
                elif kind == "o":
                    b, hh = divmod(key[0], H)
                    last = nc.vector.tensor_copy(oT[b][:, hh, :], bank[0:DV, 0:N])
                elif kind == "y":
                    n = key[0]
                    r = TP if n else B * NT
                    dve.wait_ge(bout_added, NTILES)
                    last = nc.vector.tensor_tensor(h[0:r, n, :], bank[0:r, 0:D], h[0:r, n, :], ALU.add)
                elif kind == "f2":
                    n = key[0]
                    r = TP if n else B * NT
                    wait_filled(dve, "x2T", n)
                    last = nc.vector.tensor_tensor(xn[0:r, n, :], bank[0:r, 0:D], h[0:r, n, :], ALU.add)
                last.then_inc(emptied["V"], 1)

                if kind == "peak":
                    wait_emptied(dve, "peak")
                    nc.vector.tensor_scalar(srow[:, 2:4], srow[:, 0:2], 1e-8, 1.0 / QMAX, ALU.max,
                                            ALU.mult).then_inc(scale_found, 1)
                    dve.wait_ge(scale_found, 1)
                    nc.vector.tensor_tensor(srow[:, 6:7], srow[:, 2:3], srow[:, 3:4], ALU.mult).then_inc(scale_found, 1)
                    nc.vector.reciprocal(srow[:, 4:6], srow[:, 2:4]).then_inc(scale_found, 1)
                elif kind == "scale":
                    wait_emptied(dve, "scale")
                    pieces = [(wf, 1)] + [(xf[:, :, b * NP:(b + 1) * NP], 0) for b in range(B)]

                    def divide(src, s):
                        nc.vector.tensor_scalar(src, src, scales[0:KP, s:s + 1], QMAX, ALU.mult,
                                                ALU.min).then_inc(x_scaled, 1)

                    def shift(n):
                        dve.wait_ge(x_scaled, n + 1)
                        src = pieces[n][0]
                        nc.vector.tensor_scalar(src, src, -QMAX, ROUND, ALU.max, ALU.add).then_inc(x_shifted, 1)

                    divide(*pieces[0])
                    divide(*pieces[1])
                    shift(0)
                    shift(1)
                    divide(*pieces[2])
                    shift(2)
                elif kind == "tok" and key[0] == 2:
                    dve.wait_ge(ld["txt"], 16)
                    wait_zeroed(dve, "h")
                    wait_emptied(dve, "tok", 2)
                    moments(0, (0, 1, 2))
                    normalise(0, (0, 1, 2))
                elif kind == "tok" and key[0] == NTILES - 1:
                    wait_emptied(dve, "tok", NTILES - 1)
                    moments(1, (3, 4))
                    normalise(1, (3, 4))
                elif kind == "a":
                    b = key[0]
                    wait_emptied(dve, "a", b)
                    nc.vector.tensor_copy(a3[:, :, NB:2 * NB], arow[:]).then_inc(a_step, 1)
                    dve.wait_ge(a_step, 3 * b + 2)
                    nc.vector.tensor_tensor(a3[:, :, 2 * NB:3 * NB], arow[:], a3[:, :, NB:2 * NB],
                                            ALU.subtract).then_inc(a_step, 1)
                elif kind == "s" and key[0] >= 1:
                    reciprocal(key[0] - 1)
                    if key[0] == G - 1:
                        reciprocal(G - 1)
                    if key[0] == LN_AT:
                        wait_emptied(dve, "y", 2)
                        moments(2, (1, 2))
                    elif key[0] == LN_AT + 2:
                        normalise(2, (1, 2))
                elif kind == "y" and key[0] == 0:
                    wait_emptied(dve, "y", 0)
                    moments(3, (3, 4, 0))
                    normalise(3, (3, 4, 0))

        @block.tensor
        def _(pe):
            def keep_warm(bank, times):
                for _ in range(times):
                    nc.tensor.matmul(bank, warm[:, 0:128], warm[:], start=True, stop=True)

            pe.wait_ge(warm_set, 1)
            for i, (kind, key, eng) in enumerate(items):
                bank = psum[:, i % 8, :]
                if i >= 8:
                    pe.wait_ge(emptied[items[i - 8][2]], emptied_upto[i - 8])
                keep_warm(bank, WARM.get((kind, *key), 0))
                if kind == "posg":
                    pe.wait_ge(ld["pos"], 32)
                    for p in range(PAIRS):
                        last = nc.tensor.matmul(bank[:, p * NB:(p + 1) * NB], wpos_s[:, p * 128:(p + 1) * 128],
                                                bsum[:], start=True, stop=True)
                elif kind == "peak":
                    pe.wait_ge(ld["id"], 16)
                    pe.wait_ge(peak_found, KT + 1)
                    for n in range(KT + 1):
                        last = nc.tensor.matmul(bank[0:1, n * KP:(n + 1) * KP], peaks[:, n:n + 1], idf[0:KP, 0:KP],
                                                start=True, stop=True)
                elif kind == "scale":
                    pe.wait_ge(ones_set, 1)
                    pe.wait_ge(scale_found, 3)
                    last = nc.tensor.matmul(bank[:, 0:3], ones[:], srow[:, 4:7], start=True, stop=True)
                elif kind == "tok":
                    n = key[0]
                    b = (n - 1) // 2
                    pe.wait_ge(x_rounded, 2 + b)
                    for k in range(KT):
                        last = nc.tensor.matmul(bank[:, 0:D], x8[:, k, (n - 1) * TP:n * TP], w8[:, k, :],
                                                start=(k == 0), stop=(k == KT - 1))
                elif kind in ("xnT", "x2T"):
                    n = key[0]
                    r = TP if n else B * NT
                    wait_normed(pe, 1 if kind == "xnT" else 2, n)
                    for k in range(KT):
                        last = nc.tensor.transpose(bank[0:KP, k * TP:k * TP + r], xn[0:r, n, k * KP:(k + 1) * KP],
                                                   idf[0:r, 0:r])
                elif kind in ("q", "k"):
                    b, p = key
                    w_s = wq_s if kind == "q" else wk_s
                    pe.wait_ge(ld["w" + kind], 16)
                    if kind == "k":
                        wait_zeroed(pe, "kz")
                    wait_emptied(pe, "xnT", 2 * b + 2)
                    for k in range(KT):
                        last = nc.tensor.matmul(bank[:, 0:N], w_s[:, k, p * 128:(p + 1) * 128],
                                                xnT[:, k, b * N:b * N + N], start=(k == 0), stop=(k == KT - 1))
                elif kind == "v":
                    n, half = key
                    pe.wait_ge(ld["wv"], 16)
                    for k in range(KT):
                        w_k = wv_s[:, k, half * VW:(half + 1) * VW]
                        parts = [(0, TP, cols_of(n)[:, k])] if n else [
                            (b * NT, NT, xnT[:, k, b * N + NP:(b + 1) * N]) for b in range(B)]
                        for r0, rows, x_cols in parts:
                            last = nc.tensor.matmul(bank[r0:r0 + rows, 0:VW], x_cols, w_k,
                                                    start=(k == 0), stop=(k == KT - 1))
                elif kind == "a":
                    b = key[0]
                    wait_emptied(pe, "posg")
                    for p in range(PAIRS):
                        wait_emptied(pe, "q", b, p)
                    for t in range(JT):
                        for p in range(PAIRS):
                            c0, o0 = b * N + ATILE[t], t * H * NB + p * 2 * NB
                            last = nc.tensor.matmul(bank[:, o0:o0 + 2 * NB], qp[:, p, c0:c0 + TP], gpos[:, p, :],
                                                    start=True, stop=True)
                elif kind == "aT":
                    b, t = key
                    pe.wait_ge(id_cast, 1)
                    wait_zeroed(pe, "a3")
                    pe.wait_ge(a_step, 3 * b + 3)
                    bb = bank[0:KA, :].bitcast(BF16)
                    for hh in range(H):
                        last = nc.tensor.transpose(bb[:, hh * TP:(hh + 1) * TP], a3[:, t * H + hh, :], idb[:])
                elif kind == "T":
                    b, c = key
                    pe.wait_ge(mask_cast, 1)
                    wait_emptied(pe, "aT", b, min(c // (TP // U), 2))
                    first = N - 1 - (U * c + U - 1)
                    last = nc.tensor.matmul(bank[:, 0:TW], aT[:, c, :], mask[:, first:first + TW],
                                            start=True, stop=True)
                elif kind == "s":
                    b, n = divmod(key[0], PER)
                    t, hh = tiles[n]
                    heads = [hh] if t < 2 else range(4 * hh, 4 * hh + 4)
                    rows = TP if t < 2 else NT
                    c0 = b * N + t * TP
                    for q, head in enumerate(heads):
                        wait_emptied(pe, "q", b, head // 2)
                        wait_emptied(pe, "k", b, head // 2)
                    for q, head in enumerate(heads):
                        last = nc.tensor.matmul(bank[q * rows:(q + 1) * rows, 0:N], qc[:, head // 2, c0:c0 + rows],
                                                kz[:, head, b * N:b * N + N], start=True, stop=True)
                elif kind == "x":
                    g = key[0]
                    wait_zeroed(pe, f"att{g // PER}")
                    pe.wait_ge(weights_done, g + 1)
                    e = att_tile(g)
                    for j in range(JT):
                        last = nc.tensor.transpose(bank[:, j * TP:(j + 1) * TP], e[:, j * TP:(j + 1) * TP], idf[:])
                elif kind == "o":
                    bh = key[0]
                    b, hh = divmod(bh, H)
                    for n, (t, head) in enumerate(tiles):
                        if (t < 2 and head == hh) or (t == 2 and head == hh // 4):
                            wait_emptied(pe, "x", b * PER + n)
                    for n in (0, 2 * b + 1, 2 * b + 2):
                        for half in range(VH):
                            wait_emptied(pe, "v", n, half)
                    for j in range(JT):
                        last = nc.tensor.matmul(bank[0:DV, 0:N], v[:, b * JT + j, hh * DV:(hh + 1) * DV],
                                                attT[:, bh % RING, j, :], start=(j == 0), stop=(j == JT - 1))
                elif kind == "y":
                    n = key[0]
                    pe.wait_ge(ld["wo"], 16)
                    for bh in range(B * H if n in (0, 3, 4) else H):
                        wait_emptied(pe, "o", bh)
                    for hh in range(H):
                        if n:
                            b, c0 = (n - 1) // 2, (n - 1) % 2 * TP
                            last = nc.tensor.matmul(bank[:, 0:D], oT[b][:, hh, c0:c0 + TP], wo_s[:, hh, :],
                                                    start=(hh == 0), stop=(hh == H - 1))
                        else:
                            for b in range(B):
                                last = nc.tensor.matmul(bank[b * NT:(b + 1) * NT, 0:D], oT[b][:, hh, NP:N],
                                                        wo_s[:, hh, :], start=(hh == 0), stop=(hh == H - 1))
                elif kind == "f1":
                    group, m = key
                    pe.wait_ge(ld["w1"], 16)
                    wait_emptied(pe, "x2T", (2, 4, 0)[group])
                    width = NP if group < 2 else B * NT
                    for k in range(KT):
                        x_cols = xnT[:, k, group * N:group * N + NP] if group < 2 else cols_of(0)[:, k]
                        last = nc.tensor.matmul(bank[:, 0:width], w1_s[:, k, m * 128:(m + 1) * 128], x_cols,
                                                start=(k == 0), stop=(k == KT - 1))
                elif kind == "f2":
                    n = key[0]
                    pe.wait_ge(ld["w2"], 16)
                    group = (n - 1) // 2 if n else 2
                    r, c0 = (TP, (n - 1) % 2 * TP) if n else (B * NT, 0)
                    for m in range(HID):
                        wait_emptied(pe, "f1", group, m)
                        last = nc.tensor.matmul(bank[0:r, 0:D], hidden[group][:, m, c0:c0 + r], w2_s[:, m, :],
                                                start=(m == 0), stop=(m == HID - 1))
                last.then_inc(filled, 1)


def kernel(x, txt, L0_tok_w, L0_tok_b, L0_attn_Wq, L0_attn_Wk, L0_attn_Wv, L0_attn_Wout, L0_attn_bout,
           L0_attn_Wpos, L0_attn_rel_content_bias, L0_attn_rel_pos_bias, L0_ffn_in_weight, L0_ffn_in_bias,
           L0_ffn_out_weight):
    import numpy as np
    import concourse.bacc as bacc
    from concourse import mybir as my
    from concourse.bass_utils import run_bass_kernel_spmd

    def a(v):
        return np.asarray(v)

    def chunks(m, size):
        return m.reshape(m.shape[0] // size, size, m.shape[1]).transpose(1, 0, 2)

    B, C, HH, WW = x.shape
    D, _, P, _ = L0_tok_w.shape
    gh, gw = HH // P, WW // P
    F = L0_attn_Wpos.shape[0]
    HIDDEN = L0_ffn_in_weight.shape[0]
    N = gh * gw + txt.shape[1]
    KP = 96
    H = L0_attn_rel_content_bias.shape[1]

    patches = a(x).reshape(B, C, gh, P, gw, P).transpose(1, 3, 5, 0, 2, 4).reshape(C * P * P, B * gh * gw)
    wpat = a(L0_tok_w).reshape(D, C * P * P).transpose(1, 0)
    cols = np.concatenate([
        a(L0_attn_rel_content_bias).reshape(-1, 128).transpose(1, 0),
        a(L0_attn_rel_pos_bias).reshape(-1, 128).transpose(1, 0),
        a(L0_ffn_in_bias).reshape(-1, 128).transpose(1, 0)], axis=1)
    narrow = [f for f in range(1, F + 1) if 2 ** f - 1 < N]
    nb = len(narrow) + 1
    bucket_sum = np.zeros((F, nb), np.float32)
    for f in range(1, F + 1):
        bucket_sum[f - 1, min(f, nb) - 1] = 1.0
    rel = np.abs(np.arange(-(N - 1), N))
    bucket_mask = np.zeros((3, nb, 2 * N - 1), np.float32)
    for f in range(1, nb + 1):
        bucket_mask[:, f - 1, :] = np.where(rel < 2 ** f - 1, 1.0, 0.0)
    ins = {
        "xpat": chunks(patches, KP), "txt": a(txt), "wpat": chunks(wpat, KP), "tok_b": a(L0_tok_b),
        "wq": chunks(a(L0_attn_Wq), KP), "wk": chunks(a(L0_attn_Wk), KP), "wv": chunks(a(L0_attn_Wv), KP),
        "wout": chunks(a(L0_attn_Wout), L0_attn_Wout.shape[0] // H), "bout": a(L0_attn_bout),
        "wpos": a(L0_attn_Wpos), "cols": cols,
        "w1": chunks(a(L0_ffn_in_weight).transpose(1, 0), KP), "w2": chunks(a(L0_ffn_out_weight), 128),
        "ident": np.eye(128, dtype=np.float32), "bucket_sum": bucket_sum,
        "bucket_mask": bucket_mask.reshape(3 * nb, 2 * N - 1),
    }
    nc = bacc.Bacc("TRN2", target_bir_lowering=False, num_devices=1)
    arrays, args = {}, []
    for name, arr in ins.items():
        arr = np.ascontiguousarray(arr)
        arrays["in_" + name] = arr
        args.append(nc.dram_tensor("in_" + name, arr.shape, my.dt.from_np(arr.dtype), kind="ExternalInput").ap())
    out = nc.dram_tensor("out_h", (B, N, D), my.dt.float32, kind="ExternalOutput").ap()
    early_fusion_kernel(nc, *args, out)
    r = run_bass_kernel_spmd(nc, [arrays], core_ids=[0])
    return r.results[0]["out_h"]
```

```python
from contextlib import ExitStack

import concourse.bass as bass
from concourse import mybir

F32 = mybir.dt.float32
BF16 = mybir.dt.bfloat16
ALU = mybir.AluOpType
ACT = mybir.ActivationFunctionType
AX_X = mybir.AxisListType.X

QMAX = 127.0
ROUND = 1.5 * 2.0 ** 23
BIG = 3.0e38
EPS = 1e-5
O_FIRST, O_STEP = 3, 2
WARM = {("peak",): 9, ("scale",): 3, ("tok", 1): 6, ("vt", 0): 2}


def attention_tiles(H):
    tiles = []
    for g in range(H // 4):
        tiles.append((2, g))
        tiles += [(t, h) for t in range(2) for h in range(4 * g, 4 * g + 4)]
    return tiles


def plan_items(B, H, PAIRS, CHUNKS, HID, VH, LAG):
    items = []
    turn = [0]

    def add(kind, *key, eng=None):
        if eng is None:
            eng = "AV"[turn[0] % 2]
            turn[0] += 1
        items.append((kind, key, eng))

    tiles = attention_tiles(H)
    per = len(tiles)
    chunks = list(range(CHUNKS - 2, CHUNKS)) + list(range(CHUNKS - 2))

    add("peak", eng="V")
    add("scale", eng="V")
    add("posg", eng="A")
    for n in range(1, 1 + 2 * B):
        add("tok", n, eng="V")
    add("xnT", 0, eng="A")
    add("vt", 0, eng="A")
    add("wa", eng="A")
    for n in (1, 2):
        add("xnT", n, eng="A")
    add("vt", 1, eng="V")
    add("ta", eng="V")
    for n in (1, 2):
        add("v", n, VH - 1, eng="V")
    for n in (3, 4):
        add("xnT", n, eng="A")
    add("q", 0, 0)
    rest = [("q", 0, p) for p in range(1, PAIRS)] + [("k", 0, p) for p in range(PAIRS)]
    rest += [("v", n, 0) for n in (1, 2)] + [("v", n, VH - 1) for n in (3, 4)]
    rest += [("q", 1, p) for p in range(PAIRS)] + [("k", 1, p) for p in range(PAIRS)] + [("v", n, 0) for n in (3, 4)]

    def add_rest():
        it = rest.pop(0)
        add(*it, eng="V" if it[0] == "v" and it[2] == VH - 1 else None)

    for n in range(3):
        add("aT", n)
        add_rest()
    for n, c in enumerate(chunks):
        add("T", 0, c)
        if n % 3 != 2:
            add_rest()
    for n in (3, 4):
        add("aT", n)
    waiting = [("T", 1, c) for c in chunks]
    while len(rest) > 3:
        add(*waiting.pop(0))
        add_rest()

    G = B * per
    early = {per + LAG + 8: ("y", 1), per + LAG + 9: ("y", 2), G + LAG - 4: ("x2T", 1), G + LAG - 3: ("x2T", 2)}
    engines = {"y": "V", "x2T": "A", "f1": "A", "f2": "V"}
    ready = []
    for g in range(G + LAG):
        if g < G:
            add("s", g, eng="V")
        if waiting:
            add(*waiting.pop(0))
        if rest and g % 2:
            add(*rest.pop(0))
        if g >= LAG:
            b, n = divmod(g - LAG, per)
            t, h = tiles[n]
            add("x", g - LAG)
            if t < 2 and h % 4 == 3:
                add("xt", b, h // 4, t)
            if ready and ready[0][0] <= g:
                add("o", *ready.pop(0)[1:])
            if t == 1 and h % 4 == 3:
                ready += [(g + O_FIRST + O_STEP * c, b * H // 4 + h // 4, c) for c in range(3)]
        if g in early:
            add(*early[g], eng=engines[early[g][0]])
    f1 = [("f1", 0, m) for m in range(HID)]
    tail = []
    for _, *chunk in ready:
        tail += [f1.pop(0), ("o", *chunk)]
    tail.append(f1.pop(0))
    tail += [("y", 0), ("y", 3), ("y", 4)] + f1
    tail += [("f2", 1), ("x2T", 3), ("x2T", 4), ("x2T", 0), ("f2", 2)]
    tail += [("f1", 1, m) for m in range(HID)] + [("f2", 3), ("f2", 0), ("f2", 4)]
    for it in tail:
        add(*it, eng=engines.get(it[0]))
    return items


def early_fusion_kernel(nc, xpat, txt, wpat, tok_b, wq, wqT, wk, wv, wout, bout, wpos, cols, w1, w2,
                        ident, bucket_mask, out):
    KP, KT, BP = xpat.shape
    B, NT, D = txt.shape
    NP = BP // B
    N = NP + NT
    TP = 128
    NTILES = 1 + 2 * B
    HDK = wq.shape[2]
    PAIRS = HDK // 128
    DK = 64
    H = HDK // DK
    HDV = wv.shape[2]
    DV = HDV // H
    HID = w1.shape[2] // 128
    F = wpos.shape[0]
    NB = wpos.shape[1] - HDK
    REL = 2 * N - 1
    SPLIT = 3
    BIAS = KP
    KA = 96
    U = 16
    CHUNKS = N // U
    TW = N + U - 1
    PITCH = 2 * N
    GRP = 2
    NGRP = CHUNKS // GRP
    SLOTS = 5
    VH = 2
    VW = HDV // VH
    LAG = 4
    RING = 8
    OC = HDV // 128
    JT = 3
    tiles = attention_tiles(H)
    PER = len(tiles)
    G = B * PER
    assert NP == 2 * TP and NT == 32 and U * H == 128 and SPLIT * NB <= KA and H % 4 == 0 and B == 2

    items = plan_items(B, H, PAIRS, CHUNKS, HID, VH, LAG)
    index = {(kind, *key): i for i, (kind, key, _) in enumerate(items)}
    order = [key[1] for kind, key, _ in items if kind == "T" and key[0] == 0]
    group_of = {c: n // GRP for n, c in enumerate(order)}

    with ExitStack() as ctx:
        def sb(name, shape, dt=F32):
            return ctx.enter_context(nc.sbuf_tensor(name, shape, dt))

        def sem(name):
            return ctx.enter_context(nc.semaphore(name))

        psum = ctx.enter_context(nc.psum_tensor("psum", [128, 8, 512], F32))
        skew = [nc.dram_tensor(f"skew{b}", [H, N, PITCH], F32, kind="Internal") for b in range(B)]

        early = sb("early", [128, max(KT * BP + KT * D, HID * NP)])
        xf = early[0:KP, 0:KT * BP].rearrange("p (k n) -> p k n", k=KT)
        wf = early[0:KP, KT * BP:KT * BP + KT * D].rearrange("p (k n) -> p k n", k=KT)
        idf = sb("idf", [128, 128])
        idb = sb("idb", [128, 128], BF16)
        warm = sb("warm", [128, 512], BF16)
        act_dummy = sb("act_dummy", [1, 1])
        ones = sb("ones", [1, TP])
        peaks = sb("peaks", [KP, 4])
        srow = sb("srow", [1, 8])
        scales = sb("scales", [TP, 3])
        tokb = sb("tokb", [TP, D])
        boutb = sb("boutb", [TP, D])
        colv = sb("colv", [128, cols.shape[1]])
        wq_s = sb("wq_s", [KP, KT, HDK])
        wk_s = sb("wk_s", [KP, KT, HDK])
        wqT_s = sb("wqT_s", [128, PAIRS, D + 1])
        wv_s = sb("wv_s", [KP + 1, KT, HDV + H * NB])
        wo_s = sb("wo_s", [128, OC, D])
        w1_s = sb("w1_s", [KP, KT, HID * 128])
        w2_s = sb("w2_s", [128, HID, D])
        posw = sb("posw", [F, HDK + NB])
        mask = sb("mask", [KA, REL + 1], BF16)
        gpos = sb("gpos", [128, PAIRS, 2 * NB])
        h = sb("h", [TP, NTILES, D])
        xn = sb("xn", [TP, NTILES, D])
        upper = sb("upper", [B * NT, D])
        stats = sb("stats", [TP, NTILES, 6])
        meanvar = sb("meanvar", [TP, NTILES, 2])
        vareps = sb("vareps", [TP, NTILES])
        neghalf = sb("neghalf", [TP, NTILES])
        rstd = sb("rstd", [TP, NTILES])
        xnT1 = sb("xnT1", [KP + 1, KT, B * N])
        xnT = xnT1[0:KP, :, :]
        qc = sb("qc", [128, PAIRS, B * N])
        kz = sb("kz", [128, H, B * N])
        v = sb("v", [TP, B * JT, HDV])
        arow = sb("arow", [TP, NTILES, H, NB])
        a3 = sb("a3", [TP, NTILES, H, KA], BF16)
        aT = sb("aT", [KA, B, CHUNKS, 128], BF16)
        tpos = sb("tpos", [128, SLOTS * GRP, TW])
        att = sb("att", [TP, B, PER, N])
        textw = sb("textw", [TP, B * 2 * H // 4, 128])
        nmax = sb("nmax", [TP, G])
        esum = sb("esum", [TP, G])
        rsum = sb("rsum", [TP, G])
        attT = sb("attT", [TP, RING, 2, N])
        attX = sb("attX", [TP, 2, N])
        oT = [a3[:].rearrange("p n h k -> p (n h k)").bitcast(F32)[:, 0:OC * N].rearrange("p (c n) -> p c n", c=OC),
              sb("oT1", [128, OC, N])]
        attT_flat = attT[:].rearrange("p r j n -> p (r j n)")
        x8 = attT_flat[0:KP, 0:KT * BP // 2].bitcast(BF16).rearrange("p (k n) -> p k n", k=KT)
        w8 = attT_flat[0:KP, KT * BP // 2:KT * (BP + D) // 2].bitcast(BF16).rearrange("p (k n) -> p k n", k=KT)
        maskf = attT_flat[0:SPLIT * NB, KT * (BP + D) // 2:KT * (BP + D) // 2 + REL]
        qc_flat = qc[:].rearrange("p a n -> p (a n)")
        hidden = [early[:, 0:HID * NP].rearrange("p (m n) -> p m n", m=HID),
                  qc_flat[:, 0:HID * (N + NT)].rearrange("p (m n) -> p m n", m=HID)]

        filled = sem("filled")
        emptied = {"A": sem("emptied_by_act"), "V": sem("emptied_by_dve")}
        ld = {n: sem("ld_" + n) for n in ("x0", "x1", "w", "id", "tokb", "bout", "txt", "cols", "pos", "mask", "wq",
                                          "wqT", "wk", "wv", "wo", "w1", "w2")}
        peak_found = sem("peak_found")
        scale_found = sem("scale_found")
        x_scaled = sem("x_scaled")
        x_shifted = sem("x_shifted")
        x_rounded = sem("x_rounded")
        warm_set = sem("warm_set")
        zeroed = sem("zeroed")
        kz_half = sem("kz_half")
        id_cast = sem("id_cast")
        mask_cast = sem("mask_cast")
        ones_set = sem("ones_set")
        ln_step = sem("ln_step")
        var_ready = sem("var_ready")
        rstd_ready = sem("rstd_ready")
        text_normed = sem("text_normed")
        xn_ready = sem("xn_ready")
        bout_added = sem("bout_added")
        a_step = sem("a_step")
        tpos_out = [sem(f"tpos_out{i}") for i in range(B * NGRP)]
        pos_in = [sem(f"pos_in{i}") for i in range(B * 3)]
        text_sum = sem("text_sum")
        exp_done = sem("exp_done")
        recip_done = sem("recip_done")
        weights_done = sem("weights_done")
        out_done = sem("out_done")

        zero_order = ["gpos", "bias", "h", "a3", "mask", "v", "kz"]
        norm_order = [(1, n) for n in range(1, NTILES)] + [(2, n) for n in (1, 2, 3, 4, 0)]
        root_ranges = [(0, 1), (1, 3), (3, NTILES), (1, 3), (0, NTILES)]

        emptied_upto = []
        count = {"A": 0, "V": 0}
        for _, _, e in items:
            count[e] += 1
            emptied_upto.append(count[e])

        def wait_filled(eng, *key):
            eng.wait_ge(filled, index[key] + 1)

        def wait_emptied(eng, *key):
            i = index[key]
            eng.wait_ge(emptied[items[i][2]], emptied_upto[i])

        def wait_zeroed(eng, what):
            eng.wait_ge(zeroed, zero_order.index(what) + 1)

        def wait_normed(eng, which, n):
            if (which, n) == (1, 0):
                eng.wait_ge(text_normed, 1)
                return
            eng.wait_ge(xn_ready, norm_order.index((which, n)) + 1)

        def att_tile(g):
            b, n = divmod(g, PER)
            t, hh = tiles[n]
            return att[:, b, t * H + hh, :]

        def cols_of(tile):
            if tile == 0:
                return xnT[:].rearrange("p k (b n) -> p k b n", b=B)[:, :, :, NP:N]
            return xnT[:, :, first_query(tile):first_query(tile) + TP]

        def first_query(tile):
            return (tile - 1) // 2 * N + (tile - 1) % 2 * TP

        def weights_upto(g):
            return sum(1 if tiles[n % PER][0] == 2 else 2 for n in range(g + 1))

        def empty_weights(copy, eng, g, bank):
            b, n = divmod(g, PER)
            t, hh = tiles[n]
            nth, q = divmod(b * H + hh, 4) if t < 2 else (b * H // 4 + hh, 3)
            if nth >= 2:
                wait_filled(eng, "o", nth - 2, min(q, 2))
            if t < 2:
                return copy(attT[:, (b * H + hh) % RING, :, t * TP:(t + 1) * TP],
                            bank[:, 0:2 * TP].rearrange("p (j n) -> p j n", j=2))
            r0 = (b * H + 4 * hh) % RING
            copy(attT[:, r0:r0 + 4, :, NP:N], bank[:, 0:2 * TP].rearrange("p (j h n) -> p h j n", j=2, h=4))
            slot = (b * H // 4 + hh) % 2
            for q in range(4):
                done = copy(attX[q * NT:(q + 1) * NT, slot, NP:N],
                            bank[0:NT, 2 * TP + q * NT:2 * TP + (q + 1) * NT])
            return done

        def empty_text_weights(copy, eng, b, grp, t, bank):
            nth = b * H // 4 + grp
            if nth >= 2:
                wait_filled(eng, "o", nth - 2, 2)
            return copy(attX[:, nth % 2, t * TP:(t + 1) * TP], bank[:, 0:TP])

        def empty_bands(copy, eng, n, bank):
            rows = TP if n else B * NT
            src = bank[0:KA, 0:H * rows // 2].bitcast(BF16).rearrange("p (h c u) -> p h c u", h=H, u=U)
            c = rows // U // (1 if n else B)
            for i, b in enumerate([(n - 1) // 2] if n else range(B)):
                c0 = (n - 1) % 2 * c if n else NP // U
                dst = aT[:, b, c0:c0 + c, :].rearrange("p c (u h) -> p h c u", h=H)
                done = copy(dst, src[:, :, i * c:(i + 1) * c, :])
            return done

        def empty_tpos(copy, eng, b, c, bank):
            n = b * NGRP + group_of[c]
            if n >= SLOTS:
                eng.wait_ge(tpos_out[n - SLOTS], 16 * GRP)
            return copy(tpos[:, n % SLOTS * GRP + order.index(c) % GRP, :], bank[:, 0:TW])

        def empty_v(copy, eng, n, half, bank):
            vs = slice(half * VW, (half + 1) * VW)
            return copy(v[:, (n - 1) // 2 * JT + (n - 1) % 2, vs], bank[:, 0:VW])

        def empty_v_text(copy, eng, b, bank):
            wait_zeroed(eng, "v")
            for q in range(4):
                rows = slice(q * NT, (q + 1) * NT)
                chunks_of = v[rows, b * JT + 2, :].rearrange("p (a c d) -> p a c d", c=3, d=128)
                src = bank[rows, 0:HDV // 4].rearrange("p (a d) -> p a d", d=DV)
                if q < 3:
                    done = copy(chunks_of[:, :, q, 0:DV], src)
                else:
                    done = copy(chunks_of[:, :, :, DV:128], src.rearrange("p a (c d) -> p a c d", c=3))
            return done

        LN_AT = sum(kind == "s" for kind, _, _ in items[:index["y", 2]])

        ctx.enter_context(nc.allow_non_contiguous_dma(reason="rows of a few hundred bytes"))
        block = ctx.enter_context(nc.Block())

        @block.sync
        def _(sp):
            sp.dma_start(xf[:, 0, :], xpat[:, 0, :]).then_inc(ld["x0"], 16)
            sp.dma_start(wf, wpat).then_inc(ld["w"], 16)
            sp.dma_start(wqT_s[:], wqT).then_inc(ld["wqT"], 16)
            sp.dma_start(wv_s[0:KP, :, 0:HDV], wv).then_inc(ld["wv"], 16)
            sp.dma_start(maskf, bucket_mask).then_inc(ld["mask"], 16)
            sp.dma_start(wq_s[:], wq).then_inc(ld["wq"], 16)
            sp.dma_start(colv[:], cols).then_inc(ld["cols"], 16)
            sp.dma_start(wk_s[:], wk).then_inc(ld["wk"], 16)
            sp.dma_start(boutb[:], bout.partition_broadcast(TP)).then_inc(ld["bout"], 16)
            sp.dma_start(wo_s[:], wout).then_inc(ld["wo"], 16)
            sp.dma_start(w1_s[:], w1).then_inc(ld["w1"], 16)
            sp.dma_start(w2_s[:], w2).then_inc(ld["w2"], 16)

            def send(b, grp):
                chunks = order[GRP * grp:GRP * grp + GRP]
                for c in chunks:
                    wait_emptied(sp, "T", b, c)
                slot = (b * NGRP + grp) % SLOTS
                for n, c in enumerate(chunks):
                    first = N - 1 - (U * c + U - 1)
                    dst = bass.AP(skew[b], U * c * PITCH + first, [[PITCH, U], [N * PITCH, H], [1, TW]])
                    sp.dma_start(dst, tpos[:, slot * GRP + n, :]).then_inc(tpos_out[b * NGRP + grp], 16)

            def fetch(b, t):
                for c in range(t * TP // U, min(CHUNKS, (t + 1) * TP // U)):
                    sp.wait_ge(tpos_out[b * NGRP + group_of[c]], 16 * GRP)
                start = t * TP * PITCH + N - 1 - t * TP
                if t < 2:
                    src = bass.AP(skew[b], start, [[PITCH - 1, TP], [N * PITCH, H], [1, N]])
                    sp.dma_start(att[:, b, t * H:(t + 1) * H, 0:N], src).then_inc(pos_in[b * 3 + t], 16)
                    return
                for q in range(4):
                    src = bass.AP(skew[b], start + q * N * PITCH, [[PITCH - 1, NT], [4 * N * PITCH, H // 4], [1, N]])
                    sp.dma_start(att[q * NT:(q + 1) * NT, b, 2 * H:2 * H + H // 4, 0:N],
                                 src).then_inc(pos_in[b * 3 + 2], 16)

            for b in range(B):
                for grp in range(NGRP):
                    send(b, grp)
                    if grp == 1:
                        fetch(b, 2)
                    if grp == 5:
                        fetch(b, 0)
                fetch(b, 1)
            for n in (1, 2, 3, 0, 4):
                wait_emptied(sp, "f2", n)
                if n:
                    b, t = divmod(n - 1, 2)
                    sp.dma_start(out[b, t * TP:(t + 1) * TP, :], xn[:, n, :]).then_inc(out_done, 16)
                else:
                    for b in range(B):
                        sp.dma_start(out[b, NP:N, :], xn[b * NT:(b + 1) * NT, 0, :]).then_inc(out_done, 16)
            sp.wait_ge(out_done, 16 * (NTILES - 1 + B))

        @block.gpsimd
        def _(pool):
            nc.gpsimd.memset(ones[:], 1.0).then_inc(ones_set, 1)
            nc.gpsimd.memset(neghalf[:], -0.5).then_inc(ones_set, 1)
            nc.gpsimd.memset(gpos[:], 0.0).then_inc(zeroed, 1)
            pool.wait_ge(zeroed, 1)
            nc.gpsimd.memset(xnT1[BIAS:BIAS + 1, 0, :], 1.0)
            nc.gpsimd.memset(wv_s[BIAS:BIAS + 1, 0, 0:HDV], 0.0).then_inc(zeroed, 1)
            wait_zeroed(pool, "bias")
            nc.gpsimd.memset(h[B * NT:TP, 0, :], 0.0).then_inc(zeroed, 1)
            wait_zeroed(pool, "h")
            nc.gpsimd.memset(a3[:, :, :, SPLIT * NB:KA], 0.0).then_inc(zeroed, 1)
            nc.gpsimd.memset(mask[:], 0.0).then_inc(zeroed, 1)
            pool.wait_ge(ld["id"], 16)
            nc.gpsimd.tensor_copy(idb[:], idf[:]).then_inc(id_cast, 1)

            def root(nth):
                pool.wait_ge(var_ready, nth + 1)
                a, z = root_ranges[nth]
                nc.gpsimd.tensor_tensor(rstd[:, a:z], vareps[:, a:z], neghalf[:, a:z],
                                        ALU.pow).then_inc(rstd_ready, 1)

            pool.wait_ge(ones_set, 2)
            root(0)
            pool.wait_ge(rstd_ready, 1)
            nc.gpsimd.tensor_scalar(xn[:, 0, :], h[:, 0, :], meanvar[:, 0, 0:1], rstd[:, 0:1],
                                    ALU.subtract, ALU.mult).then_inc(text_normed, 1)
            nc.gpsimd.memset(v[:].rearrange("p (b j) n -> p b j n", j=JT)[:, :, 2, :], 0.0).then_inc(zeroed, 1)
            wait_zeroed(pool, "v")
            kz2 = kz[:].rearrange("p (a two) n -> p a two n", two=2)
            nc.gpsimd.memset(kz2[0:64, :, 1, :], 0.0).then_inc(kz_half, 1)
            pool.wait_ge(kz_half, 1)
            root(1)
            root(2)
            pool.wait_ge(rstd_ready, 3)
            nc.gpsimd.memset(kz2[64:128, :, 0, :], 0.0).then_inc(zeroed, 1)
            wait_zeroed(pool, "kz")
            pool.wait_ge(ld["bout"], 16)
            for n in range(NTILES):
                wait_normed(pool, 1, n)
                nc.gpsimd.tensor_tensor(h[:, n, :], h[:, n, :], boutb[:], ALU.add).then_inc(bout_added, 1)
            for g in range(G):
                if g == LN_AT:
                    root(3)
                pool.wait_ge(recip_done, g + 1)
                e = att_tile(g)
                b, n = divmod(g, PER)
                t, hh = tiles[n]
                if t < 2:
                    grp, q = divmod(hh, 4)
                    nc.gpsimd.tensor_scalar(textw[:, (b * H // 4 + grp) * 2 + t, q * NT:(q + 1) * NT], e[:, NP:N],
                                            rsum[:, g:g + 1], 1.0, ALU.mult, ALU.mult).then_inc(weights_done, 1)
                    e = e[:, 0:NP]
                nc.gpsimd.tensor_scalar(e, e, rsum[:, g:g + 1], 1.0, ALU.mult, ALU.mult).then_inc(weights_done, 1)
            root(4)

        @block.scalar
        def _(act):
            act.dma_start(xf[:, 1, :], xpat[:, 1, :]).then_inc(ld["x1"], 16)
            act.dma_start(idf[:], ident).then_inc(ld["id"], 16)
            act.dma_start(h[0:B * NT, 0, :], txt.rearrange("b n d -> (b n) d")).then_inc(ld["txt"], 16)
            act.dma_start(posw[:], wpos).then_inc(ld["pos"], 16)
            act.dma_start(tokb[:], tok_b.partition_broadcast(TP)).then_inc(ld["tokb"], 16)
            act.wait_ge(warm_set, 2)
            nc.scalar.activation(act_dummy[:], act_dummy[:], ACT.Copy, bias=0.0)

            act.wait_ge(x_shifted, 1)
            nc.scalar.activation(w8, wf, ACT.Copy, bias=-ROUND).then_inc(x_rounded, 1)
            for b in range(B):
                act.wait_ge(x_shifted, 2 + b)
                nc.scalar.activation(x8[:, :, b * NP:(b + 1) * NP], xf[:, :, b * NP:(b + 1) * NP], ACT.Copy,
                                     bias=-ROUND).then_inc(x_rounded, 1)

            for i, (kind, key, eng) in enumerate(items):
                bank = psum[:, i % 8, :]
                if kind == "s":
                    g = key[0]
                    wait_emptied(act, "s", g)
                    e = att_tile(g)
                    nc.scalar.activation(e, e, ACT.Exp, bias=nmax[:, g:g + 1], scale=-1.0,
                                         accum_out=esum[:, g:g + 1]).then_inc(exp_done, 1)
                if eng != "A":
                    continue
                act.wait_ge(filled, i + 1)
                if kind in ("xnT", "x2T"):
                    src = bank[0:KP, 0:KT * TP].rearrange("p (k n) -> p k n", k=KT)
                    if key[0] == 0:
                        src = src[:, :, 0:B * NT].rearrange("p k (b n) -> p k b n", b=B)
                    last = nc.scalar.copy(cols_of(key[0]), src)
                elif kind == "q":
                    b, p = key
                    cs = slice(b * N, b * N + N)
                    act.wait_ge(ld["cols"], 16)
                    last = nc.scalar.activation(qc[:, p, cs], bank[:, 0:N], ACT.Identity, bias=colv[:, p:p + 1],
                                                scale=DK ** -0.5)
                elif kind == "posg":
                    wait_zeroed(act, "gpos")
                    g2 = bank[:, 0:PAIRS * NB].rearrange("p (a f) -> p a f", a=PAIRS)
                    nc.scalar.copy(gpos[0:64, :, 0:NB], g2[0:64])
                    last = nc.scalar.copy(gpos[64:128, :, NB:2 * NB], g2[64:128])
                elif kind == "wa":
                    src = bank[:, 0:KT * H * NB].rearrange("p (k f) -> p k f", k=KT)
                    nc.scalar.activation(wv_s[0:KP, :, HDV:], src[0:KP], ACT.Copy, scale=DK ** -0.5)
                    last = nc.scalar.copy(wv_s[BIAS:BIAS + 1, 0, HDV:], src[BIAS:BIAS + 1, 0, :])
                elif kind == "k":
                    b, p = key
                    cs = slice(b * N, b * N + N)
                    nc.scalar.copy(kz[0:64, 2 * p, cs], bank[0:64, 0:N])
                    last = nc.scalar.copy(kz[64:128, 2 * p + 1, cs], bank[64:128, 0:N])
                elif kind == "v":
                    last = empty_v(nc.scalar.copy, act, *key, bank)
                elif kind == "aT":
                    last = empty_bands(nc.scalar.copy, act, *key, bank)
                elif kind == "T":
                    last = empty_tpos(nc.scalar.copy, act, *key, bank)
                elif kind == "vt":
                    last = empty_v_text(nc.scalar.copy, act, *key, bank)
                elif kind == "x":
                    last = empty_weights(nc.scalar.copy, act, key[0], bank)
                elif kind == "xt":
                    last = empty_text_weights(nc.scalar.copy, act, *key, bank)
                elif kind == "o":
                    b, a = divmod(key[0], H // 4)
                    last = nc.scalar.copy(oT[b][:, 3 * a + key[1], :], bank[:, 0:N])
                elif kind == "f1":
                    group, m = key
                    c = PAIRS + m
                    last = nc.scalar.activation(hidden[group][:, m, :], bank[:, 0:hidden[group].shape[2]], ACT.Gelu,
                                                bias=colv[:, c:c + 1])
                last.then_inc(emptied["A"], 1)
                if (kind, *key) == ("xnT", NTILES - 1):
                    act.wait_ge(ld["mask"], 16)
                    wait_zeroed(act, "mask")
                    nc.scalar.copy(mask[0:SPLIT * NB, 0:REL], maskf).then_inc(mask_cast, 1)

        @block.vector
        def _(dve):
            nc.vector.memset(warm[:], 0.0).then_inc(warm_set, 1)
            nc.vector.memset(act_dummy[:], 0.0).then_inc(warm_set, 1)
            for k in range(KT):
                dve.wait_ge(ld[f"x{k}"], 16)
                nc.vector.tensor_reduce(peaks[:, k:k + 1], xf[:, k, :], AX_X, ALU.max,
                                        apply_absolute_value=True).then_inc(peak_found, 1)
            dve.wait_ge(peak_found, KT)
            nc.vector.tensor_tensor(peaks[:, 2:3], peaks[:, 0:1], peaks[:, 1:2], ALU.max).then_inc(peak_found, 1)
            dve.wait_ge(ld["w"], 16)
            nc.vector.tensor_reduce(peaks[:, 3:4], early[0:KP, KT * BP:KT * BP + KT * D], AX_X, ALU.max,
                                    apply_absolute_value=True).then_inc(peak_found, 1)
            ln = [0]

            def ln_done(ins):
                ln[0] += 1
                ins.then_inc(ln_step, 1)
                dve.wait_ge(ln_step, ln[0])

            def moments(nth, group):
                for n in group:
                    last = nc.vector.bn_stats(stats[:, n, :], h[:, n, :])
                ln_done(last)
                for n in group:
                    last = nc.vector.bn_aggr(meanvar[:, n, :], stats[:, n, :])
                ln_done(last)
                a, z = root_ranges[nth]
                nc.vector.tensor_scalar(vareps[:, a:z], meanvar[:, a:z, 1], EPS, None, ALU.add).then_inc(var_ready, 1)

            def normalise(nth, group):
                dve.wait_ge(rstd_ready, nth + 1)
                for n in group:
                    nc.vector.tensor_scalar(xn[:, n, :], h[:, n, :], meanvar[:, n, 0:1], rstd[:, n:n + 1],
                                            ALU.subtract, ALU.mult).then_inc(xn_ready, 1)

            dve.wait_ge(ld["txt"], 16)
            wait_zeroed(dve, "h")
            nc.vector.bn_stats(stats[:, 0, :], h[:, 0, :]).then_inc(ln_step, 1)
            ln[0] += 1

            def reciprocal(g):
                dve.wait_ge(exp_done, g + 1)
                nc.vector.reciprocal(rsum[:, g:g + 1], esum[:, g:g + 1]).then_inc(recip_done, 1)

            for i, (kind, key, eng) in enumerate(items):
                if eng != "V":
                    continue
                bank = psum[:, i % 8, :]
                dve.wait_ge(filled, i + 1)
                if kind == "peak":
                    last = nc.vector.tensor_reduce(srow[:, 0:2], bank[0:1, 0:2 * KP].rearrange("p (s n) -> p s n", s=2),
                                                   AX_X, ALU.max)
                elif kind == "scale":
                    last = nc.vector.tensor_copy(scales[:], bank[:, 0:3])
                elif kind == "tok":
                    n = key[0]
                    if n == 1:
                        dve.wait_ge(ld["tokb"], 16)
                    last = nc.vector.scalar_tensor_tensor(out=h[:, n, :], in0=bank[:, 0:D], scalar=scales[:, 2:3],
                                                          in1=tokb[:], op0=ALU.mult, op1=ALU.add)
                elif kind == "q":
                    b, p = key
                    cs = slice(b * N, b * N + N)
                    dve.wait_ge(ld["cols"], 16)
                    last = nc.vector.tensor_scalar(qc[:, p, cs], bank[:, 0:N], DK ** -0.5, colv[:, p:p + 1],
                                                   ALU.mult, ALU.add)
                elif kind == "k":
                    b, p = key
                    cs = slice(b * N, b * N + N)
                    nc.vector.tensor_copy(kz[0:64, 2 * p, cs], bank[0:64, 0:N])
                    last = nc.vector.tensor_copy(kz[64:128, 2 * p + 1, cs], bank[64:128, 0:N])
                elif kind == "ta" or (kind == "v" and key[1] == VH - 1):
                    n, rows, c0 = (key[0], TP, VW) if kind == "v" else (0, B * NT, 0)
                    src = bank[0:rows, c0:c0 + H * NB].rearrange("p (h f) -> p h f", f=NB)
                    part = a3[0:rows, n]
                    rest = arow[0:rows, n]
                    nc.vector.tensor_copy(part[:, :, 0:NB], src).then_inc(a_step, 1)
                    if kind == "v":
                        empty_v(nc.vector.tensor_copy, dve, *key, bank)
                    dve.wait_ge(a_step, 3 * n + 1)
                    last = nc.vector.tensor_tensor(rest, src, part[:, :, 0:NB], ALU.subtract)
                elif kind == "v":
                    last = empty_v(nc.vector.tensor_copy, dve, *key, bank)
                elif kind == "aT":
                    last = empty_bands(nc.vector.tensor_copy, dve, *key, bank)
                elif kind == "T":
                    last = empty_tpos(nc.vector.tensor_copy, dve, *key, bank)
                elif kind == "s":
                    g = key[0]
                    b, n = divmod(g, PER)
                    dve.wait_ge(pos_in[b * 3 + tiles[n][0]], 16 * (4 if tiles[n][0] == 2 else 1))
                    e = att_tile(g)
                    last = nc.vector.tensor_tensor_reduce(e, bank[:, 0:N], e, -1.0, BIG, ALU.add, ALU.min,
                                                          nmax[:, g:g + 1])
                elif kind == "vt":
                    last = empty_v_text(nc.vector.tensor_copy, dve, *key, bank)
                elif kind == "x":
                    last = empty_weights(nc.vector.tensor_copy, dve, key[0], bank)
                elif kind == "xt":
                    last = empty_text_weights(nc.vector.tensor_copy, dve, *key, bank)
                elif kind == "o":
                    b, a = divmod(key[0], H // 4)
                    last = nc.vector.tensor_copy(oT[b][:, 3 * a + key[1], :], bank[:, 0:N])
                elif kind in ("y", "f2"):
                    n = key[0]
                    r = TP if n else B * NT
                    if kind == "y":
                        dve.wait_ge(bout_added, NTILES)
                        dst = h[0:r, n, :]
                    else:
                        wait_filled(dve, "x2T", n)
                        dst = xn[0:r, n, :]
                    if n:
                        last = nc.vector.tensor_tensor(dst, bank[:, 0:D], h[:, n, :], ALU.add)
                    else:
                        sums = 2 * (kind == "f2")
                        nc.vector.tensor_copy(upper[:], bank[r:2 * r, 0:D]).then_inc(text_sum, 1)
                        dve.wait_ge(text_sum, sums + 1)
                        nc.vector.tensor_tensor(upper[:], upper[:], h[0:r, n, :], ALU.add).then_inc(text_sum, 1)
                        dve.wait_ge(text_sum, sums + 2)
                        last = nc.vector.tensor_tensor(dst, bank[0:r, 0:D], upper[:], ALU.add)
                last.then_inc(emptied["V"], 1)

                if kind == "peak":
                    wait_emptied(dve, "peak")
                    nc.vector.tensor_scalar(srow[:, 2:4], srow[:, 0:2], 1e-8, 1.0 / QMAX, ALU.max,
                                            ALU.mult).then_inc(scale_found, 1)
                    dve.wait_ge(scale_found, 1)
                    nc.vector.tensor_tensor(srow[:, 6:7], srow[:, 2:3], srow[:, 3:4], ALU.mult).then_inc(scale_found, 1)
                    nc.vector.reciprocal(srow[:, 4:6], srow[:, 2:4]).then_inc(scale_found, 1)
                    dve.wait_ge(ln_step, ln[0])
                    ln_done(nc.vector.bn_aggr(meanvar[:, 0, :], stats[:, 0, :]))
                    nc.vector.tensor_scalar(vareps[:, 0:1], meanvar[:, 0:1, 1], EPS, None,
                                            ALU.add).then_inc(var_ready, 1)
                elif kind == "scale":
                    wait_emptied(dve, "scale")
                    pieces = [(wf, 1)] + [(xf[:, :, b * NP:(b + 1) * NP], 0) for b in range(B)]

                    def divide(src, s):
                        nc.vector.tensor_scalar(src, src, scales[0:KP, s:s + 1], QMAX, ALU.mult,
                                                ALU.min).then_inc(x_scaled, 1)

                    def shift(n):
                        dve.wait_ge(x_scaled, n + 1)
                        src = pieces[n][0]
                        nc.vector.tensor_scalar(src, src, -QMAX, ROUND, ALU.max, ALU.add).then_inc(x_shifted, 1)

                    divide(*pieces[0])
                    divide(*pieces[1])
                    shift(0)
                    shift(1)
                    divide(*pieces[2])
                    shift(2)
                elif kind == "tok" and key[0] == 2:
                    wait_emptied(dve, "tok", 2)
                    moments(1, (1, 2))
                elif kind == "tok" and key[0] == NTILES - 1:
                    wait_emptied(dve, "tok", NTILES - 1)
                    normalise(1, (1, 2))
                    moments(2, (3, 4))
                    normalise(2, (3, 4))
                elif kind == "ta" or (kind == "v" and key[1] == VH - 1):
                    wait_emptied(dve, kind, *key)
                    nc.vector.tensor_copy(part[:, :, NB:2 * NB], rest).then_inc(a_step, 1)
                    dve.wait_ge(a_step, 3 * n + 2)
                    nc.vector.tensor_tensor(part[:, :, 2 * NB:3 * NB], rest, part[:, :, NB:2 * NB],
                                            ALU.subtract).then_inc(a_step, 1)
                elif kind == "s" and key[0] >= 1:
                    reciprocal(key[0] - 1)
                    if key[0] == G - 1:
                        reciprocal(G - 1)
                    if key[0] == LN_AT:
                        wait_emptied(dve, "y", 2)
                        moments(3, (1, 2))
                    elif key[0] == LN_AT + 2:
                        normalise(3, (1, 2))
                elif kind == "y" and key[0] == 4:
                    wait_emptied(dve, "y", 4)
                    moments(4, (3, 4, 0))
                    normalise(4, (3, 4, 0))

        @block.tensor
        def _(pe):
            def keep_warm(bank, times):
                for _ in range(times):
                    nc.tensor.matmul(bank, warm[:, 0:128], warm[:], start=True, stop=True)

            pe.wait_ge(warm_set, 1)
            for i, (kind, key, eng) in enumerate(items):
                bank = psum[:, i % 8, :]
                if i >= 8:
                    pe.wait_ge(emptied[items[i - 8][2]], emptied_upto[i - 8])
                keep_warm(bank, WARM.get((kind, *key), 0))
                if kind == "posg":
                    pe.wait_ge(ld["pos"], 16)
                    for p in range(PAIRS):
                        last = nc.tensor.matmul(bank[:, p * NB:(p + 1) * NB], posw[:, p * 128:(p + 1) * 128],
                                                posw[:, HDK:HDK + NB], start=True, stop=True)
                elif kind == "peak":
                    pe.wait_ge(ld["id"], 16)
                    pe.wait_ge(peak_found, KT + 2)
                    for n in range(2):
                        last = nc.tensor.matmul(bank[0:1, n * KP:(n + 1) * KP], peaks[:, 2 + n:3 + n], idf[0:KP, 0:KP],
                                                start=True, stop=True)
                elif kind == "wa":
                    pe.wait_ge(ld["wqT"], 16)
                    wait_emptied(pe, "posg")
                    for k in range(KT):
                        first, rows = (0, KP + 1) if k == 0 else (KP + 1, KP)
                        for p in range(PAIRS):
                            c0 = (k * PAIRS + p) * 2 * NB
                            last = nc.tensor.matmul(bank[0:rows, c0:c0 + 2 * NB], wqT_s[:, p, first:first + rows],
                                                    gpos[:, p, :], start=True, stop=True)
                elif kind == "ta":
                    wait_emptied(pe, "xnT", 0)
                    wait_emptied(pe, "wa")
                    wait_zeroed(pe, "bias")
                    for k in range(KT):
                        rows = KP + 1 if k == 0 else KP
                        for b in range(B):
                            last = nc.tensor.matmul(bank[b * NT:(b + 1) * NT, 0:H * NB],
                                                    xnT1[0:rows, k, b * N + NP:(b + 1) * N], wv_s[0:rows, k, HDV:],
                                                    start=(k == 0), stop=(k == KT - 1))
                elif kind == "scale":
                    pe.wait_ge(ones_set, 1)
                    pe.wait_ge(scale_found, 3)
                    last = nc.tensor.matmul(bank[:, 0:3], ones[:], srow[:, 4:7], start=True, stop=True)
                elif kind == "tok":
                    n = key[0]
                    b = (n - 1) // 2
                    pe.wait_ge(x_rounded, 2 + b)
                    for k in range(KT):
                        last = nc.tensor.matmul(bank[:, 0:D], x8[:, k, (n - 1) * TP:n * TP], w8[:, k, :],
                                                start=(k == 0), stop=(k == KT - 1))
                elif kind in ("xnT", "x2T"):
                    n = key[0]
                    r = TP if n else B * NT
                    wait_normed(pe, 1 if kind == "xnT" else 2, n)
                    for k in range(KT):
                        last = nc.tensor.transpose(bank[0:KP, k * TP:k * TP + r], xn[0:r, n, k * KP:(k + 1) * KP],
                                                   idf[0:r, 0:r])
                elif kind in ("q", "k"):
                    b, p = key
                    w_s = wq_s if kind == "q" else wk_s
                    pe.wait_ge(ld["w" + kind], 16)
                    if kind == "k":
                        wait_zeroed(pe, "kz")
                    wait_emptied(pe, "xnT", 2 * b + 2)
                    for k in range(KT):
                        last = nc.tensor.matmul(bank[:, 0:N], w_s[:, k, p * 128:(p + 1) * 128],
                                                xnT[:, k, b * N:b * N + N], start=(k == 0), stop=(k == KT - 1))
                elif kind == "v":
                    n, half = key
                    pe.wait_ge(ld["wv"], 16)
                    wait_emptied(pe, "xnT", n)
                    if half == VH - 1:
                        wait_emptied(pe, "wa")
                        wait_zeroed(pe, "bias")
                    for k in range(KT):
                        last_half = half == VH - 1
                        rows = KP + 1 if last_half and k == 0 else KP
                        width = VW + (H * NB if last_half else 0)
                        last = nc.tensor.matmul(bank[:, 0:width],
                                                xnT1[0:rows, k, first_query(n):first_query(n) + TP],
                                                wv_s[0:rows, k, half * VW:half * VW + width],
                                                start=(k == 0), stop=(k == KT - 1))
                elif kind == "vt":
                    b = key[0]
                    pe.wait_ge(ld["wv"], 16)
                    wait_emptied(pe, "xnT", 0)
                    w4 = wv_s[0:KP, :, 0:HDV].rearrange("p k (a q d) -> p k q a d", q=4, d=DV)
                    for k in range(KT):
                        for q in range(4):
                            last = nc.tensor.matmul(
                                bank[q * NT:(q + 1) * NT, 0:HDV // 4].rearrange("p (a d) -> p a d", d=DV),
                                xnT[:, k, b * N + NP:(b + 1) * N], w4[:, k, q], start=(k == 0), stop=(k == KT - 1))
                elif kind == "aT":
                    n = key[0]
                    rows = TP if n else B * NT
                    pe.wait_ge(id_cast, 1)
                    wait_zeroed(pe, "a3")
                    pe.wait_ge(a_step, 3 * n + 3)
                    bb = bank[0:KA, :].bitcast(BF16)
                    for hh in range(H):
                        last = nc.tensor.transpose(bb[:, hh * rows:(hh + 1) * rows], a3[0:rows, n, hh, :],
                                                   idb[0:rows, 0:rows])
                elif kind == "T":
                    b, c = key
                    pe.wait_ge(mask_cast, 1)
                    wait_emptied(pe, "aT", 2 * b + 1 + c // (TP // U) if c < NP // U else 0)
                    first = N - 1 - (U * c + U - 1)
                    last = nc.tensor.matmul(bank[:, 0:TW], aT[:, b, c, :], mask[:, first:first + TW],
                                            start=True, stop=True)
                elif kind == "s":
                    b, n = divmod(key[0], PER)
                    t, hh = tiles[n]
                    heads = [hh] if t < 2 else range(4 * hh, 4 * hh + 4)
                    rows = TP if t < 2 else NT
                    c0 = b * N + t * TP
                    for q, head in enumerate(heads):
                        wait_emptied(pe, "q", b, head // 2)
                        wait_emptied(pe, "k", b, head // 2)
                    for q, head in enumerate(heads):
                        last = nc.tensor.matmul(bank[q * rows:(q + 1) * rows, 0:N], qc[:, head // 2, c0:c0 + rows],
                                                kz[:, head, b * N:b * N + N], start=True, stop=True)
                elif kind == "x":
                    g = key[0]
                    pe.wait_ge(weights_done, weights_upto(g))
                    e = att_tile(g)
                    for j in range(2):
                        last = nc.tensor.transpose(bank[:, j * TP:(j + 1) * TP], e[:, j * TP:(j + 1) * TP], idf[:])
                    if tiles[g % PER][0] == 2:
                        last = nc.tensor.transpose(bank[0:NT, 2 * TP:3 * TP], e[:, NP:N], idf[:])
                elif kind == "xt":
                    b, grp, t = key
                    pe.wait_ge(weights_done, weights_upto(b * PER + tiles.index((t, 4 * grp + 3))))
                    last = nc.tensor.transpose(bank[:, 0:TP], textw[:, (b * H // 4 + grp) * 2 + t, :], idf[:])
                elif kind == "o":
                    nth, c = key
                    b, a = divmod(nth, H // 4)
                    for n, (t, head) in enumerate(tiles):
                        if (t < 2 and head // 4 == a) or (t == 2 and head == a):
                            wait_emptied(pe, "x", b * PER + n)
                    for t in range(2):
                        wait_emptied(pe, "xt", b, a, t)
                        wait_emptied(pe, "v", 2 * b + 1 + t, 4 * a * VH // H)
                    wait_emptied(pe, "vt", b)
                    parts = [(0, 64, 4 * a + c, 0), (64, 32, 4 * a + c, 64), (96, 32, 4 * a + 3, 32 * c)]
                    for j in range(2):
                        for p0, width, hh, d0 in parts:
                            d0 += hh * DV
                            nc.tensor.matmul(bank[p0:p0 + width, 0:N], v[:, b * JT + j, d0:d0 + width],
                                             attT[:, (b * H + hh) % RING, j, :], start=(j == 0), stop=False)
                    c0 = (3 * a + c) * 128
                    last = nc.tensor.matmul(bank[:, 0:N], v[:, b * JT + 2, c0:c0 + 128], attX[:, nth % 2, :],
                                            start=False, stop=True)
                elif kind == "y":
                    n = key[0]
                    pe.wait_ge(ld["wo"], 16)
                    for nth in range(B * H // 4 if n in (0, 3, 4) else H // 4):
                        for c in range(3):
                            wait_emptied(pe, "o", nth, c)
                    for c in range(OC if n else OC // 2):
                        if n:
                            b, c0 = (n - 1) // 2, (n - 1) % 2 * TP
                            last = nc.tensor.matmul(bank[:, 0:D], oT[b][:, c, c0:c0 + TP], wo_s[:, c, :],
                                                    start=(c == 0), stop=(c == OC - 1))
                        else:
                            for q in range(2 * B):
                                half, b = divmod(q, B)
                                last = nc.tensor.matmul(bank[q * NT:(q + 1) * NT, 0:D],
                                                        oT[b][:, half * OC // 2 + c, NP:N],
                                                        wo_s[:, half * OC // 2 + c, :],
                                                        start=(c == 0), stop=(c == OC // 2 - 1))
                elif kind == "f1":
                    group, m = key
                    pe.wait_ge(ld["w1"], 16)
                    wait_emptied(pe, "x2T", (2, 0)[group])
                    c0, width = (0, NP) if group == 0 else (NP, N + NT)
                    for k in range(KT):
                        last = nc.tensor.matmul(bank[:, 0:width], w1_s[:, k, m * 128:(m + 1) * 128],
                                                xnT[:, k, c0:c0 + width], start=(k == 0), stop=(k == KT - 1))
                elif kind == "f2":
                    n = key[0]
                    pe.wait_ge(ld["w2"], 16)
                    group = n in (3, 4, 0)
                    if n:
                        c0 = (0 if group == 0 else NT) + (n - 1) % 2 * TP
                        for m in range(HID):
                            wait_emptied(pe, "f1", group, m)
                            last = nc.tensor.matmul(bank[:, 0:D], hidden[group][:, m, c0:c0 + TP], w2_s[:, m, :],
                                                    start=(m == 0), stop=(m == HID - 1))
                    else:
                        for m in range(HID // 2):
                            wait_emptied(pe, "f1", group, HID // 2 + m)
                            for q in range(2 * B):
                                half, b = divmod(q, B)
                                last = nc.tensor.matmul(bank[q * NT:(q + 1) * NT, 0:D],
                                                        hidden[group][:, half * HID // 2 + m, b * N:b * N + NT],
                                                        w2_s[:, half * HID // 2 + m, :],
                                                        start=(m == 0), stop=(m == HID // 2 - 1))
                last.then_inc(filled, 1)


def kernel(x, txt, L0_tok_w, L0_tok_b, L0_attn_Wq, L0_attn_Wk, L0_attn_Wv, L0_attn_Wout, L0_attn_bout,
           L0_attn_Wpos, L0_attn_rel_content_bias, L0_attn_rel_pos_bias, L0_ffn_in_weight, L0_ffn_in_bias,
           L0_ffn_out_weight):
    import numpy as np
    import concourse.bacc as bacc
    from concourse import mybir as my
    from concourse.bass_utils import run_bass_kernel_spmd

    def a(v):
        return np.asarray(v)

    def chunks(m, size):
        return m.reshape(m.shape[0] // size, size, m.shape[1]).transpose(1, 0, 2)

    B, C, HH, WW = x.shape
    D, _, P, _ = L0_tok_w.shape
    gh, gw = HH // P, WW // P
    F = L0_attn_Wpos.shape[0]
    HIDDEN = L0_ffn_in_weight.shape[0]
    N = gh * gw + txt.shape[1]
    KP = 96
    H = L0_attn_rel_content_bias.shape[1]

    patches = a(x).reshape(B, C, gh, P, gw, P).transpose(1, 3, 5, 0, 2, 4).reshape(C * P * P, B * gh * gw)
    wpat = a(L0_tok_w).reshape(D, C * P * P).transpose(1, 0)
    cols = np.concatenate([
        a(L0_attn_rel_content_bias).reshape(-1, 128).transpose(1, 0),
        a(L0_ffn_in_bias).reshape(-1, 128).transpose(1, 0)], axis=1)
    wqT = a(L0_attn_Wq).transpose(1, 0)
    wqT = np.concatenate([wqT[:, 0:KP], a(L0_attn_rel_pos_bias).reshape(-1, 1), wqT[:, KP:]], axis=1)
    w = a(L0_attn_Wout).reshape(H // 4, 4, 3, 32, D)
    wout = np.concatenate([w[:, 0:3].reshape(H // 4, 3, 96, D), w[:, 3]], axis=2).reshape(-1, 128, D).transpose(1, 0, 2)
    narrow = [f for f in range(1, F + 1) if 2 ** f - 1 < N]
    nb = len(narrow) + 1
    bucket_sum = np.zeros((F, nb), np.float32)
    for f in range(1, F + 1):
        bucket_sum[f - 1, min(f, nb) - 1] = 1.0
    rel = np.abs(np.arange(-(N - 1), N))
    bucket_mask = np.zeros((3, nb, 2 * N - 1), np.float32)
    for f in range(1, nb + 1):
        bucket_mask[:, f - 1, :] = np.where(rel < 2 ** f - 1, 1.0, 0.0)
    ins = {
        "xpat": chunks(patches, KP), "txt": a(txt), "wpat": chunks(wpat, KP), "tok_b": a(L0_tok_b),
        "wq": chunks(a(L0_attn_Wq), KP), "wqT": chunks(wqT, 128),
        "wk": chunks(a(L0_attn_Wk), KP), "wv": chunks(a(L0_attn_Wv), KP),
        "wout": wout, "bout": a(L0_attn_bout),
        "wpos": np.concatenate([a(L0_attn_Wpos), bucket_sum], axis=1), "cols": cols,
        "w1": chunks(a(L0_ffn_in_weight).transpose(1, 0), KP), "w2": chunks(a(L0_ffn_out_weight), 128),
        "ident": np.eye(128, dtype=np.float32),
        "bucket_mask": bucket_mask.reshape(3 * nb, 2 * N - 1),
    }
    nc = bacc.Bacc("TRN2", target_bir_lowering=False, num_devices=1)
    arrays, args = {}, []
    for name, arr in ins.items():
        arr = np.ascontiguousarray(arr)
        arrays["in_" + name] = arr
        args.append(nc.dram_tensor("in_" + name, arr.shape, my.dt.from_np(arr.dtype), kind="ExternalInput").ap())
    out = nc.dram_tensor("out_h", (B, N, D), my.dt.float32, kind="ExternalOutput").ap()
    early_fusion_kernel(nc, *args, out)
    r = run_bass_kernel_spmd(nc, [arrays], core_ids=[0])
    return r.results[0]["out_h"]
```
